# Optimizing a Trainium2 kernel written in Bass

```python
import numpy as np
import jax
import jax.numpy as jnp

def _softmax(x, axis=-1):
    return jax.nn.softmax(x, axis=axis)

def _gelu(x):
    return jax.nn.gelu(x, approximate=True)

def _silu(x):
    return jax.nn.silu(x)

def _sigmoid(x):
    return jax.nn.sigmoid(x)

def _layernorm(x, axis=-1, eps=1e-05):
    m = jnp.mean(x, axis=axis, keepdims=True)
    v = jnp.var(x, axis=axis, keepdims=True)
    return (x - m) / jnp.sqrt(v + eps)

def _scatter_add(tgt, idx, src, axis=0):
    return tgt.at[idx].add(src)

def _segment_sum(src, seg, n):
    return jax.ops.segment_sum(src, seg, n)
kernel_name = 'mk_decoder_postln_d1_seqx_r8_633494'

def setup_inputs(seed: int=0):
    np.random.seed(seed)
    _w = jnp.asarray

    def _rec_inputs():
        import jax
        import jax.numpy as jnp
        _rk = jax.random.key(seed)
        x = -0.0002928 + 1 * jax.random.normal(jax.random.fold_in(_rk, 1), (32, 128, 128), jnp.float32)
        _lenS = 128 - jax.random.randint(jax.random.fold_in(_rk, 7), (32,), 0, max(1, 128 // 4) + 1, jnp.int32)
        _lenS2 = 77 - jax.random.randint(jax.random.fold_in(_rk, 8), (32,), 0, max(1, 77 // 4) + 1, jnp.int32)
        _ctx_1024P = jax.random.normal(jax.random.fold_in(_rk, 11), (32, 16, 128), jnp.float32)
        _ctx_1024c = jax.random.dirichlet(jax.random.fold_in(_rk, 511), 0.3 * jnp.ones((16,), jnp.float32), (32, 77))
        _ctx_1024t = jnp.einsum('bsk,bkd->bsd', _ctx_1024c, _ctx_1024P)
        _ctx_1024t = _ctx_1024t * jax.lax.rsqrt(jnp.mean(jnp.square(_ctx_1024t)) + 1e-12) * 0.953939
        ctx_1024 = 4.13588e-05 + 0.999923 * (_ctx_1024t + 0.3 * jax.random.normal(jax.random.fold_in(_rk, 611), (32, 77, 128), jnp.float32))
        return (x, ctx_1024)
    x, ctx_1024 = _rec_inputs()

    def _L0_attn_setup():
        import jax, jax.numpy as jnp
        import numpy as np
        HEADS = 16
        THETA = 10000.0

        def _rope(x):
            b, n, d = x.shape
            half = d // 2
            inv_freq = 1.0 / THETA ** (jnp.arange(0, d, 2, dtype=jnp.float32) / d)
            ang = jnp.arange(n, dtype=jnp.float32)[:, None] * inv_freq
            cos, sin = (jnp.cos(ang), jnp.sin(ang))
            xp = x.reshape(b, n, half, 2)
            x1, x2 = (xp[..., 0], xp[..., 1])
            out = jnp.stack([x1 * cos - x2 * sin, x2 * cos + x1 * sin], axis=-1)
            return out.reshape(b, n, d)
        key = jax.random.key(seed)
        ks = jax.random.split(key, 8)
        B, N, C = (8, 256, 128)
        s = C ** (-0.5)
        return {'x': jax.random.normal(ks[0], (B, N, C), jnp.float32), 'Wq': jax.random.normal(ks[1], (C, C), jnp.float32) * s, 'bq': jax.random.normal(ks[2], (C,), jnp.float32) * 0.01, 'Wk': jax.random.normal(ks[3], (C, C), jnp.float32) * s, 'bk': jax.random.normal(ks[4], (C,), jnp.float32) * 0.01, 'Wv': jax.random.normal(ks[5], (C, C), jnp.float32) * s, 'bv': jax.random.normal(ks[6], (C,), jnp.float32) * 0.01, 'gamma': jnp.ones((C,), jnp.float32), 'beta': jnp.zeros((C,), jnp.float32)}
    _L0_attn_all = _L0_attn_setup()
    _L0_attn_in = {k: v for k, v in _L0_attn_all.items() if k in ('Wq', 'bq', 'Wk', 'bk', 'Wv', 'bv', 'gamma', 'beta')}
    del _L0_attn_all

    def _L0_xattn_setup():
        import jax, jax.numpy as jnp
        import numpy as np
        import math
        EMBED_DIM = 128
        NUM_HEADS = 16
        D_K = EMBED_DIM // NUM_HEADS
        B, S_DEC, S_ENC = (4, 128, 256)
        key = jax.random.key(seed)
        ks = jax.random.split(key, 12)
        s = 1.0 / math.sqrt(EMBED_DIM)
        return {'Q_decoder': jax.random.normal(ks[0], (B, S_DEC, EMBED_DIM), jnp.float32), 'K_encoder': jax.random.normal(ks[1], (B, S_ENC, EMBED_DIM), jnp.float32), 'V_encoder': jax.random.normal(ks[2], (B, S_ENC, EMBED_DIM), jnp.float32), 'Wq': jax.random.normal(ks[3], (EMBED_DIM, EMBED_DIM), jnp.float32) * s, 'bq': jnp.zeros((EMBED_DIM,), jnp.float32), 'Wk': jax.random.normal(ks[4], (EMBED_DIM, EMBED_DIM), jnp.float32) * s, 'bk': jnp.zeros((EMBED_DIM,), jnp.float32), 'Wv': jax.random.normal(ks[5], (EMBED_DIM, EMBED_DIM), jnp.float32) * s, 'bv': jnp.zeros((EMBED_DIM,), jnp.float32), 'Wo': jax.random.normal(ks[6], (EMBED_DIM, EMBED_DIM), jnp.float32) * s, 'bo': jnp.zeros((EMBED_DIM,), jnp.float32)}
    _L0_xattn_all = _L0_xattn_setup()
    _L0_xattn_in = {k: v for k, v in _L0_xattn_all.items() if k in ('Wq', 'bq', 'Wk', 'bk', 'Wv', 'bv', 'Wo', 'bo')}
    del _L0_xattn_all

    def _L0_ffn_setup():
        import jax, jax.numpy as jnp
        import numpy as np
        E = 16
        K = 4
        B, S, H, I = (4, 128, 128, 256)
        key = jax.random.key(seed)
        k0, k1, k2, k3 = jax.random.split(key, 4)
        scale = 0.02
        return {'hidden_states': jax.random.normal(k0, (B, S, H), jnp.float32), 'router_w': jax.random.normal(k1, (H, E), jnp.float32) * scale, 'router_b': jnp.zeros((E,), jnp.float32), 'w1': jax.random.normal(k2, (E, H, I), jnp.float32) * scale, 'b1': jnp.zeros((E, I), jnp.float32), 'w2': jax.random.normal(k3, (E, I, H), jnp.float32) * scale, 'b2': jnp.zeros((E, H), jnp.float32)}
    _L0_ffn_all = _L0_ffn_setup()
    _L0_ffn_in = {k: v for k, v in _L0_ffn_all.items() if k in ('router_w', 'router_b', 'w1', 'b1', 'w2', 'b2')}
    del _L0_ffn_all
    return {'x': x, 'ctx_1024': ctx_1024, 'L0_attn_Wq': _L0_attn_in['Wq'], 'L0_attn_bq': _L0_attn_in['bq'], 'L0_attn_Wk': _L0_attn_in['Wk'], 'L0_attn_bk': _L0_attn_in['bk'], 'L0_attn_Wv': _L0_attn_in['Wv'], 'L0_attn_bv': _L0_attn_in['bv'], 'L0_attn_gamma': _L0_attn_in['gamma'], 'L0_attn_beta': _L0_attn_in['beta'], 'L0_xattn_Wq': _L0_xattn_in['Wq'], 'L0_xattn_bq': _L0_xattn_in['bq'], 'L0_xattn_Wk': _L0_xattn_in['Wk'], 'L0_xattn_bk': _L0_xattn_in['bk'], 'L0_xattn_Wv': _L0_xattn_in['Wv'], 'L0_xattn_bv': _L0_xattn_in['bv'], 'L0_xattn_Wo': _L0_xattn_in['Wo'], 'L0_xattn_bo': _L0_xattn_in['bo'], 'L0_ffn_router_w': _L0_ffn_in['router_w'], 'L0_ffn_router_b': _L0_ffn_in['router_b'], 'L0_ffn_w1': _L0_ffn_in['w1'], 'L0_ffn_b1': _L0_ffn_in['b1'], 'L0_ffn_w2': _L0_ffn_in['w2'], 'L0_ffn_b2': _L0_ffn_in['b2']}

def reference(x, ctx_1024, L0_attn_Wq, L0_attn_bq, L0_attn_Wk, L0_attn_bk, L0_attn_Wv, L0_attn_bv, L0_attn_gamma, L0_attn_beta, L0_xattn_Wq, L0_xattn_bq, L0_xattn_Wk, L0_xattn_bk, L0_xattn_Wv, L0_xattn_bv, L0_xattn_Wo, L0_xattn_bo, L0_ffn_router_w, L0_ffn_router_b, L0_ffn_w1, L0_ffn_b1, L0_ffn_w2, L0_ffn_b2):
    import jax
    import jax.numpy as jnp

    def _L0_attn_ref(x, Wq, bq, Wk, bk, Wv, bv, gamma, beta):
        import jax, jax.numpy as jnp
        import numpy as np
        HEADS = 16
        THETA = 10000.0

        def _rope(x):
            b, n, d = x.shape
            half = d // 2
            inv_freq = 1.0 / THETA ** (jnp.arange(0, d, 2, dtype=jnp.float32) / d)
            ang = jnp.arange(n, dtype=jnp.float32)[:, None] * inv_freq
            cos, sin = (jnp.cos(ang), jnp.sin(ang))
            xp = x.reshape(b, n, half, 2)
            x1, x2 = (xp[..., 0], xp[..., 1])
            out = jnp.stack([x1 * cos - x2 * sin, x2 * cos + x1 * sin], axis=-1)
            return out.reshape(b, n, d)
        b, n, c = x.shape
        h = HEADS
        d = c // h
        gelu = lambda t: jax.nn.gelu(t, approximate=False)
        q = gelu(x @ Wq.T + bq) + 0.21
        k = gelu(x @ Wk.T + bk) + 0.21
        v = x @ Wv.T + bv
        q_r = _rope(q)
        k_r = _rope(k)
        split = lambda t: t.reshape(b, n, h, d).transpose(0, 2, 1, 3)
        qh, kh, vh, qrh, krh = (split(q), split(k), split(v), split(q_r), split(k_r))
        z = 1.0 / (jnp.einsum('bhnd,bhd->bhn', qh, kh.mean(axis=2)) + 1e-06)
        scale = n ** (-0.5)
        kv = jnp.einsum('bhnd,bhne->bhde', krh * scale, vh * scale)
        out = jnp.einsum('bhnd,bhde->bhne', qrh, kv) * z[..., None]
        out = out.transpose(0, 2, 1, 3).reshape(b, n, c)
        res = out + x
        mu = res.mean(-1, keepdims=True)
        var = res.var(-1, keepdims=True)
        return (res - mu) / jnp.sqrt(var + 1e-12) * gamma + beta

    def _L0_xattn_ref(Q_decoder, K_encoder, V_encoder, Wq, bq, Wk, bk, Wv, bv, Wo, bo):
        import jax, jax.numpy as jnp
        import numpy as np
        import math
        EMBED_DIM = 128
        NUM_HEADS = 16
        D_K = EMBED_DIM // NUM_HEADS
        B, S_DEC, S_ENC = (4, 128, 256)
        b, sd, d = Q_decoder.shape
        se = K_encoder.shape[1]
        Q = (Q_decoder @ Wq + bq).reshape(b, sd, NUM_HEADS, D_K).transpose(0, 2, 1, 3)
        K = (K_encoder @ Wk + bk).reshape(b, se, NUM_HEADS, D_K).transpose(0, 2, 1, 3)
        V = (V_encoder @ Wv + bv).reshape(b, se, NUM_HEADS, D_K).transpose(0, 2, 1, 3)
        scores = jnp.einsum('bhqd,bhkd->bhqk', Q, K) / math.sqrt(D_K)
        attn = jax.nn.softmax(scores, axis=-1)
        out = jnp.einsum('bhqk,bhkd->bhqd', attn, V)
        out = out.transpose(0, 2, 1, 3).reshape(b, sd, d)
        return out @ Wo + bo

    def _L0_ffn_ref(hidden_states, router_w, router_b, w1, b1, w2, b2):
        import jax, jax.numpy as jnp
        import numpy as np
        E = 16
        K = 4
        B, S, H, I = (4, 128, 128, 256)
        b, s, h = hidden_states.shape
        logits = hidden_states @ router_w + router_b
        probs = jax.nn.softmax(logits, axis=-1)
        topw, topi = jax.lax.top_k(probs, K)
        topw = topw / jnp.sum(topw, axis=-1, keepdims=True)
        combine = jnp.sum(jax.nn.one_hot(topi, E, dtype=hidden_states.dtype) * topw[..., None], axis=2)
        x = hidden_states.reshape(b * s, h)
        c = combine.reshape(b * s, E)

        def body(acc, expert):
            w1e, b1e, w2e, b2e, ce = expert
            hmid = jax.nn.gelu(x @ w1e + b1e, approximate=False)
            return (acc + (hmid @ w2e + b2e) * ce[:, None], None)
        out, _ = jax.lax.scan(body, jnp.zeros_like(x), (w1, b1, w2, b2, c.T))
        return out.reshape(b, s, h)
    x = _layernorm(x + _L0_attn_ref(x, L0_attn_Wq, L0_attn_bq, L0_attn_Wk, L0_attn_bk, L0_attn_Wv, L0_attn_bv, L0_attn_gamma, L0_attn_beta), axis=-1)
    x = _layernorm(x + _L0_xattn_ref(x, ctx_1024, ctx_1024, L0_xattn_Wq, L0_xattn_bq, L0_xattn_Wk, L0_xattn_bk, L0_xattn_Wv, L0_xattn_bv, L0_xattn_Wo, L0_xattn_bo), axis=-1)
    x = _layernorm(x + _L0_ffn_ref(x, L0_ffn_router_w, L0_ffn_router_b, L0_ffn_w1, L0_ffn_b1, L0_ffn_w2, L0_ffn_b2), axis=-1)
    return x

_drawn_inputs = setup_inputs


def setup_inputs(seed=0):
    import zlib

    import numpy as np

    out = dict(_drawn_inputs(seed))
    spreads = {'L0_attn_gamma': (1.0, 0.2),
     'L0_attn_beta': (0.0, 0.1),
     'L0_xattn_bq': (0.0, 0.325),
     'L0_xattn_bk': (0.0, 2.0),
     'L0_xattn_bv': (0.0, 0.1),
     'L0_xattn_bo': (0.0, 0.1),
     'L0_ffn_router_b': (0.0, 0.1),
     'L0_ffn_b1': (0.0, 0.8),
     'L0_ffn_b2': (0.0, 0.1)}
    factors = {'L0_attn_bq': 33.463,
     'L0_attn_bk': 36.145,
     'L0_attn_bv': 8.0,
     'L0_ffn_w1': 3.027,
     'L0_ffn_w2': 2.712}
    for name, (base, spread) in spreads.items():
        noise = np.random.default_rng([zlib.crc32(name.encode()), seed]).standard_normal(out[name].shape)
        drawn = base * np.exp(spread * noise) if base else spread * noise
        out[name] = jnp.asarray(drawn.astype(out[name].dtype))
    for name, factor in factors.items():
        out[name] = (out[name] * factor).astype(out[name].dtype)
    return out
```

```python
from contextlib import ExitStack

import numpy as np
import concourse.bass as bass
from concourse import mybir

ALU = mybir.AluOpType
ACT = mybir.ActivationFunctionType
AX = mybir.AxisListType
F32 = mybir.dt.float32
F16 = mybir.dt.float16
BF16 = mybir.dt.bfloat16

P = 128
B = 4
SEQS = 32
GROUPS = SEQS // B
T = B * P
CTX = 77
HEADS = 16
HD = 8
BLK = 4
E = 16
HID = 256
HALF = HID // P
TOPK = 4
LAG = 3
RING = 4
WS = 256.0
FAR = -3.0e38
THETA = 10000.0


def constants():
    half = np.arange(0, P, 2, dtype=np.float32)
    inv = (np.float32(1.0) / np.float32(THETA) ** (half / np.float32(P))).astype(np.float32)
    ang = (np.arange(P, dtype=np.float32)[:, None] * inv).astype(np.float32)
    cos, sin = np.cos(ang).astype(np.float32), np.sin(ang).astype(np.float32)
    cos2, sin2 = np.repeat(cos, 2, axis=1), np.repeat(sin, 2, axis=1)
    ident = np.eye(P, dtype=np.float32)
    rot = np.zeros((P, P), np.float32)
    for i in range(0, P, 2):
        rot[i + 1, i] = -1.0
        rot[i, i + 1] = 1.0
    ch = np.arange(P)
    same_head = (ch[:, None] // HD == ch[None, :] // HD).astype(np.float32) / P
    head_of = (ch[:, None] // HD == np.arange(HEADS)[None, :]).astype(np.float32)
    part = ch // HD % 4
    q_low = -(part >= 2).astype(np.float32)[:, None]
    k_low = -(part % 2 == 1).astype(np.float32)[:, None]
    ones = np.ones((P, P), np.float32)
    pick = np.zeros((P, BLK, CTX), np.float32)
    for r in range(4):
        for hl in range(2):
            for b in range(BLK):
                pick[32 * r + 16 * hl + 4 * r + b, b] = -1.0
    cols = dict(ident=ident, rot=rot, cos=cos2, sin_neg=-sin, sin=sin, cos_t=cos2.T, sin_t=sin2.T,
                same_head=same_head, head_of=head_of, q_low=q_low, k_low=k_low, ones=ones,
                pick=pick.reshape(P, BLK * CTX))
    at, where = 0, {}
    for k, v in cols.items():
        where[k] = (at, v.shape[1])
        at += v.shape[1]
    return np.ascontiguousarray(np.concatenate(list(cols.values()), axis=1), np.float32), where


AT = dict(x_t=0, proj=1, rot=3, kv=5, out=7, k_rep=6, k_rep2=8, x1_t=11, q_rep=13,
          scores=15, per_seq=3, ao_t=28, wo=29,
          logits=1, c_t=4, b2=5)


def build(nc, A, consts, where, out):
    ctx = ExitStack()
    with ctx:
        def sb(name, shape, dt=F32):
            return ctx.enter_context(nc.sbuf_tensor(name, shape, dt))

        def sem(name):
            return ctx.enter_context(nc.semaphore(name))

        cst = sb("cst", [P, consts.shape[1]])

        def c_(name):
            a, n = where[name]
            return cst[:, a:a + n]

        ident = c_("ident")
        identb = sb("identb", [P, P], BF16)
        pick = sb("pick", [P, BLK, CTX], BF16)
        mean_col = sb("mean_col", [P, 1])
        half_pow = sb("half_pow", [P, B])
        w_in = sb("w_in", [P, 3, P])
        wq_t = sb("wq_t", [P, P])
        wkv_t = sb("wkv_t", [P, 2, P])
        xw = sb("xw", [P, 4, P])
        wq_rep = sb("wq_rep", [P, BLK, 4, 4, HD])
        wk_rep = sb("wk_rep", [P, BLK, 4, 4, HD])
        rows = sb("rows", [1, 8, P])
        rb_row = sb("rb_row", [1, E])
        rep_rows = sb("rep_rows", [1, 2, BLK, 4, 4, HD])
        wide = sb("wide", [P, 6, P])
        rb = sb("rb", [P, E])
        bq = sb("bq", [P, 1])
        b_rep = sb("b_rep", [P, 2, BLK])
        b_neg = sb("b_neg", [P, 2, BLK])
        rw = sb("rw", [P, E])
        rwh = sb("rwh", [P, E], F16)
        rwl = sb("rwl", [P, E], F16)
        b1_in = sb("b1_in", [E * HALF, P])
        b1 = sb("b1", [P, E, HALF])
        b2 = sb("b2", [E, P])
        w_stage = sb("w_stage", [P, E * HID])
        w1h = sb("w1h", [P, E, HID], F16)
        w1l = sb("w1l", [P, E, HID], F16)
        w2h = sb("w2h", [P, E, HALF, P], F16)
        w2l = sb("w2l", [P, E, HALF, P], F16)
        x = sb("x", [P, B, P])
        cx = sb("cx", [CTX, B, P])
        x_t = sb("x_t", [P, T])
        cx_t = sb("cx_t", [P, B * CTX])
        qg = sb("qg", [P, T])
        q = sb("q", [P, T])
        q_cos = sb("q_cos", [P, T])
        q_sin = sb("q_sin", [P, T])
        qr = sb("qr", [P, T])
        kb = sb("kb", [P, B, P])
        v = sb("v", [P, B, P])
        kg = sb("kg", [P, B, P])
        k_cos = sb("k_cos", [P, B, P])
        k_sin = sb("k_sin", [P, B, P])
        kr = sb("kr", [P, B, P])
        k_mean = sb("k_mean", [P, B, HEADS])
        kv = sb("kv", [P, B, P])
        den = sb("den", [P, B * HEADS])
        z = sb("z", [P, B * HEADS])
        oz = sb("oz", [P, B, P])
        res = sb("res", [P, B, P])
        x_beta = sb("x_beta", [P, B, P])
        resg = sb("resg", [P, B, P])
        y1 = sb("y1", [P, B, P])
        x1 = sb("x1", [P, B, P])
        x1_bo = sb("x1_bo", [P, B, P])
        x1_t = sb("x1_t", [P, T])
        v1 = sb("v1", [CTX, B, HEADS, HD + 1])
        k_neg = sb("k_neg", [P, BLK, B * CTX], F16)
        k_rep = sb("k_rep", [P, BLK, B * CTX], F16)
        q_neg = sb("q_neg", [P, BLK, T], F16)
        q_rep = sb("q_rep", [P, BLK, T], F16)
        mx = sb("mx", [P, 4, BLK])
        mx_hl = sb("mx_hl", [P, 4, 2, HEADS], BF16)
        mx_t = sb("mx_t", [P, P], BF16)
        prob = sb("prob", [CTX, HEADS * P])
        rs = sb("rs", [P, HEADS])
        ao = sb("ao", [P, B, P])
        ao_t = sb("ao_t", [P, T])
        y2 = sb("y2", [P, B, P])
        x2n = sb("x2n", [P, B, P])
        stats = sb("stats", [P, 4, B, 6])
        mv = sb("mv", [P, 4, B, 2])
        ve = sb("ve", [P, 4, B])
        rstd = sb("rstd", [P, 4, B])
        x2h = sb("x2h", [P, T], F16)
        x2l = sb("x2l", [P, T], F16)
        x2 = sb("x2", [P, B, P])
        lg = sb("lg", [P, B, E + 8])
        top = sb("top", [P, B, 8])
        cut = sb("cut", [P, B, E + 8])
        chosen = sb("chosen", [P, B, E])
        lgm = sb("lgm", [P, B, E])
        th = sb("th", [P, B, E])
        num = sb("num", [P, B, E])
        dnm = sb("dnm", [P, B, E])
        rdn = sb("rdn", [P, B, E])
        pe_ = sb("pe_", [P, B, E])
        pm = sb("pm", [P, B, E])
        ps_ = sb("ps_", [P, B])
        ps2 = sb("ps2", [P, B])
        rps = sb("rps", [P, B])
        cw = sb("cw", [P, B, E])
        cw_t = sb("cw_t", [E, T])
        acc = sb("acc", [P, B, P])
        g32 = sb("g32", [P, 2, HALF, T])
        gh = sb("gh", [P, RING, HALF, T], F16)
        gl = sb("gl", [P, RING, HALF, T], F16)
        fin = sb("fin", [P, B, P])

        ps = ctx.enter_context(nc.psum_tensor("ps", [P, 8, 512], F32))
        bA, bB, bC, bD, bE, bY = (ps[:, i, :] for i in range(6))
        bH = ps[:, 6:8, :]

        names = """ld_c ld_w ld_r ld_w1 ld_w2 ld_x ld_cx st_out
            i_ones i_idb i_wt i_wtc i_rows i_bc i_bcc i_rep i_brp i_brc i_bn i_b1 i_b1c i_w1h i_w1 i_w2h i_w2 i_rw i_rwl i_v1 i_lg
            x_tp x_tc cx_tp cx_tc proj kb v qg kg q rot k_mean_p kv_p k_mean k_cos k_sin kr kv q_cos q_sin qr
            d_p out_p den z oz res x_beta st1 ag1 ve1 rs1 resg y1 st2 ag2 ve2 rs2 x1 x1_bo x1_tp x1_tc
            v1_p v1 k_rep_p k_neg k_rep q_rep_p q_neg q_rep s_p mx mxh mxl mxt_p mxt_c t_p prob av_p rs_ ao
            ao_tp ao_tc wo_p y2 st3 ag3 ve3 rs3 x2n x2_tp x2h x2l x2cp
            lg_p lg top topx cut chosen lgm th num dnm rdn pe_ pm ps_ ps2 rps cw cw_tp cw_tc b2_p acc0
            h_p gelu hi lo y_p comb st4 ag4 ve4 rs4 fin""".split()
        s = {n: sem("s_" + n) for n in names}

        def since(eng, name, n):
            if not (isinstance(n, int) and n <= 0):
                eng.wait_ge(s[name], n)

        AVW = HD + 1
        x_dram = A["x"].rearrange("(g b) n c -> g n b c", b=B)
        cx_dram = A["ctx_1024"].rearrange("(g b) n c -> g n b c", b=B)
        out_dram = out.rearrange("(g b) n c -> g n b c", b=B)

        def row(name):
            return A[name].rearrange("(a n) -> a n", a=1)

        block = ctx.enter_context(nc.Block())

        @block.sync
        def _(sp):
            def load(g):
                since(sp, "res", g)
                since(sp, "x_beta", g)
                sp.dma_start(x[:, :, :], x_dram[g]).then_inc(s["ld_x"], 16)
                since(sp, "cx_tp", g)
                sp.dma_start(cx[:, :, :], cx_dram[g]).then_inc(s["ld_cx"], 16)

            def store(g):
                since(sp, "fin", g + 1)
                sp.dma_start(out_dram[g], fin[:, :, :]).then_inc(s["st_out"], 16)

            load(0)
            sp.dma_start(w_stage[:, :].rearrange("p (e n) -> p e n", e=E),
                         A["L0_ffn_w1"].rearrange("e c n -> c e n")).then_inc(s["ld_w1"], 16)
            load(1)
            with sp.Fori(0, GROUPS - 2) as it:
                load(it + 2)
                store(it)
            store(GROUPS - 2)
            store(GROUPS - 1)
            sp.wait_ge(s["st_out"], 16 * GROUPS)

        @block.gpsimd
        def _(pool):
            pool.memset(mean_col[:, :], 1.0 / P).then_inc(s["i_ones"], 1)
            pool.memset(half_pow[:, :], -0.5).then_inc(s["i_ones"], 1)
            pool.memset(v1[:, :, :, HD:HD + 1], 1.0).then_inc(s["i_v1"], 1)
            pool.memset(lg[:, :, E:E + 8], FAR).then_inc(s["i_lg"], 1)
            pool.wait_ge(s["ld_c"], 16)
            pool.tensor_copy(identb[:, :], ident).then_inc(s["i_idb"], 1)
            pool.tensor_copy(pick[:, :, :], c_("pick").rearrange("p (b k) -> p b k", b=BLK)).then_inc(s["i_idb"], 1)
            pool.wait_ge(s["ld_w"], 16 * 4)
            for rep, i in ((wq_rep, 0), (wk_rep, 1)):
                for n in range(4):
                    pool.tensor_copy(rep[:, :, :, n, :], xw[:, i, :].rearrange("p (b r d) -> p b r d", b=BLK, r=4)).then_inc(s["i_rep"], 1)
            pool.wait_ge(s["ld_r"], 16 * 14)
            for i in range(2):
                for n in range(4):
                    pool.tensor_copy(rep_rows[:, i, :, :, n, :], rows[:, 6 + i, :].rearrange("p (b r d) -> p b r d", b=BLK, r=4)).then_inc(s["i_rep"], 1)

            def power(n, g, name_ve, name_rs):
                since(pool, name_ve, g + 1)
                pool.tensor_tensor(rstd[:, n, :], ve[:, n, :], half_pow[:, :], ALU.pow).then_inc(s[name_rs], 1)

            def attention(g, p):
                if p == AT["proj"]:
                    pool.wait_ge(s["ld_x"], 16 * (g + 1))
                    since(pool, "i_bcc", 2)
                    since(pool, "y1", g)
                    pool.tensor_tensor(x_beta[:, :, :], x[:, :, :], wide[:, 3:4, :].broadcast_to([P, B, P]), ALU.add).then_inc(s["x_beta"], 1)
                if p == AT["kv"] - 1:
                    since(pool, "k_sin", 2 * (g + 1))
                    since(pool, "k_cos", g + 1)
                    since(pool, "kv_p", g)
                    pool.tensor_tensor(kr[:, :, :], k_cos[:, :, :], k_sin[:, :, :], ALU.add).then_inc(s["kr"], 1)
                if p == AT["kv"]:
                    since(pool, "q_cos", g + 1)
                    since(pool, "q_sin", g + 1)
                    since(pool, "out_p", g)
                    pool.tensor_tensor(qr[:, :], q_cos[:, :], q_sin[:, :], ALU.add).then_inc(s["qr"], 1)
                if p == AT["out"]:
                    since(pool, "oz", g + 1)
                    pool.tensor_tensor(res[:, :, :], oz[:, :, :], x[:, :, :], ALU.add).then_inc(s["res"], 1)
                    power(0, g, "ve1", "rs1")
                    power(1, g, "ve2", "rs2")
                if p == AT["x1_t"]:
                    since(pool, "x1", g + 1)
                    since(pool, "y2", g)
                    pool.tensor_tensor(x1_bo[:, :, :], x1[:, :, :], wide[:, 5:6, :].broadcast_to([P, B, P]), ALU.add).then_inc(s["x1_bo"], 1)
                if p == AT["wo"]:
                    power(2, g, "ve3", "rs3")

            def low(it, e):
                n = E * it + e
                since(pool, "hi", n + 1)
                pool.tensor_tensor(gl[:, e % RING, :, :], g32[:, e % 2, :, :], gh[:, e % RING, :, :], ALU.subtract).then_inc(s["lo"], 1)

            def body(it, g):
                for e in range(E):
                    if it is not None:
                        low(it, e)
                    for p in (2 * e, 2 * e + 1):
                        if g is not None:
                            attention(g, p)
                if it is not None:
                    power(3, it, "ve4", "rs4")

            body(None, 0)
            body(0, 1)
            with pool.Fori(1, GROUPS - 1) as it:
                body(it, it + 1)
            body(GROUPS - 1, None)

        @block.scalar
        def _(act):
            act.dma_start(cst[:, :], consts).then_inc(s["ld_c"], 16)
            for i, n in enumerate(("L0_attn_Wq", "L0_attn_Wk", "L0_attn_Wv")):
                act.dma_start(w_in[:, i, :], A[n]).then_inc(s["ld_r"], 16)
            for i, n in enumerate(("L0_xattn_Wq", "L0_xattn_Wk", "L0_xattn_Wv", "L0_xattn_Wo")):
                act.dma_start(xw[:, i, :], A[n]).then_inc(s["ld_w"], 16)
            for i, n in enumerate(("L0_attn_bk", "L0_attn_bv", "L0_attn_gamma", "L0_attn_beta", "L0_xattn_bv", "L0_xattn_bo", "L0_xattn_bq", "L0_xattn_bk")):
                act.dma_start(rows[:, i, :], row(n)).then_inc(s["ld_r"], 16)
            act.dma_start(rb_row[:, :], row("L0_ffn_router_b")).then_inc(s["ld_r"], 16)
            act.dma_start(bq[:, :], A["L0_attn_bq"].rearrange("(n a) -> n a", a=1)).then_inc(s["ld_r"], 16)
            act.dma_start(b1_in[:, :], A["L0_ffn_b1"].rearrange("e (h n) -> (e h) n", h=HALF)).then_inc(s["ld_r"], 16)
            act.dma_start(b2[:, :], A["L0_ffn_b2"]).then_inc(s["i_b1"], 16)
            act.dma_start(rw[:, :], A["L0_ffn_router_w"]).then_inc(s["i_rw"], 16)
            act.wait_ge(s["i_wt"], 1)
            act.copy(wq_t[:, :], bA[:, 0:P]).then_inc(s["i_wtc"], 1)
            act.copy(wkv_t[:, :, :], bA[:, P:3 * P].rearrange("p (i n) -> p i n", i=2)).then_inc(s["i_wtc"], 1)
            act.copy(b1[:, :, :], bA[:, 3 * P:3 * P + E * HALF].rearrange("p (e h) -> p e h", h=HALF)).then_inc(s["i_wtc"], 1)
            act.wait_ge(s["i_bc"], 1)
            act.copy(wide[:, 0:4, :], bB.rearrange("p (i n) -> p i n", i=4)).then_inc(s["i_bcc"], 1)
            act.copy(wide[:, 4:6, :], bC[:, 0:2 * P].rearrange("p (i n) -> p i n", i=2)).then_inc(s["i_bcc"], 1)
            act.copy(rb[:, :], bC[:, 2 * P:2 * P + E]).then_inc(s["i_bcc"], 1)
            act.copy(b_rep[:, :, :], bC[:, 2 * P + E:2 * P + E + 2 * BLK].rearrange("p (i n) -> p i n", i=2)).then_inc(s["i_bcc"], 1)
            act.wait_ge(s["i_rw"], 16)
            act.activation(rwh[:, :], rw[:, :], ACT.Copy, scale=WS).then_inc(s["i_rwl"], 1)

            def high_weights():
                act.wait_ge(s["ld_w1"], 16)
                act.activation(w1h[:, :, :], w_stage[:, :].rearrange("p (e n) -> p e n", e=E), ACT.Copy, scale=WS).then_inc(s["i_w1h"], 1)
                act.wait_ge(s["i_w1"], 1)
                act.dma_start(w_stage[:, :].rearrange("p (e h n) -> p e h n", e=E, h=HALF),
                              A["L0_ffn_w2"].rearrange("e (h i) n -> i e h n", h=HALF)).then_inc(s["ld_w2"], 16)
                act.wait_ge(s["ld_w2"], 16)
                act.activation(w2h[:, :, :, :], w_stage[:, :].rearrange("p (e h n) -> p e h n", e=E, h=HALF), ACT.Copy, scale=WS).then_inc(s["i_w2h"], 1)

            def attention(g, p):
                if p == AT["x_t"]:
                    since(act, "x_tp", g + 1)
                    act.copy(x_t[:, :], bA).then_inc(s["x_tc"], 1)
                    since(act, "cx_tp", g + 1)
                    act.copy(cx_t[:, :], bB[:, 0:B * CTX]).then_inc(s["cx_tc"], 1)
                if p == AT["proj"]:
                    since(act, "proj", 2 * g + 1)
                    since(act, "q", g)
                    act.activation(qg[:, :], bA, ACT.Gelu, bias=bq[:, :]).then_inc(s["qg"], 1)
                    since(act, "kb", g + 1)
                    since(act, "k_sin", 2 * g)
                    since(act, "k_mean_p", g)
                    act.activation(kg[:, :, :], kb[:, :, :], ACT.Gelu).then_inc(s["kg"], 1)
                for first, at in ((0, "k_rep"), (2, "k_rep2")):
                    if p == AT[at]:
                        since(act, "k_rep_p", 2 * g + first // 2 + 1)
                        since(act, "k_rep", 4 * g)
                        for i in (first, first + 1):
                            act.activation(k_neg[:, i, :], (bB, bC)[i % 2][:, 0:B * CTX], ACT.Identity,
                                           bias=b_neg[:, 1, i:i + 1], scale=c_("k_low")).then_inc(s["k_neg"], 1)
                if p == AT["x1_t"]:
                    since(act, "x1_tp", g + 1)
                    act.copy(x1_t[:, :], bA).then_inc(s["x1_tc"], 1)
                if p == AT["q_rep"]:
                    since(act, "q_rep_p", g + 1)
                    since(act, "q_rep", 4 * g)
                    for i in range(BLK):
                        act.activation(q_neg[:, i, :], ps[:, i, :], ACT.Identity,
                                       bias=b_neg[:, 0, i:i + 1], scale=c_("q_low")).then_inc(s["q_neg"], 1)
                for b in range(B):
                    n = B * g + b
                    at = AT["scores"] + AT["per_seq"] * b
                    if p == at + 1:
                        since(act, "mxt_p", n + 1)
                        since(act, "t_p", n)
                        act.copy(mx_t[:, :], ps[:, 4, 0:P // 2].bitcast(BF16)).then_inc(s["mxt_c"], 1)
                    if p == at + 2:
                        since(act, "t_p", n + 1)
                        since(act, "av_p", n)
                        act.activation(prob[:, :].rearrange("p (r n) -> p r n", r=4), ps[0:CTX, 0:4, :],
                                       ACT.Exp, scale=float(HD) ** -0.5).then_inc(s["prob"], 1)
                if p == AT["ao_t"]:
                    since(act, "ao_tp", g + 1)
                    act.copy(ao_t[:, :], bA).then_inc(s["ao_tc"], 1)

            def tail(g):
                since(act, "x2_tp", g + 1)
                since(act, "h_p", E * g)
                since(act, "lg_p", g)
                act.copy(x2h[:, :], bA).then_inc(s["x2h"], 1)

            def router(it, p):
                if p == AT["logits"]:
                    since(act, "lgm", it + 1)
                    act.activation(th[:, :, :], lgm[:, :, :], ACT.Tanh, scale=0.5).then_inc(s["th"], 1)
                if p == AT["c_t"]:
                    since(act, "cw_tp", it + 1)
                    act.copy(cw_t[:, :], ps[0:E, 4, :]).then_inc(s["cw_tc"], 1)

            def gelu(it, e):
                n = E * it + e
                since(act, "h_p", n + 1)
                since(act, "lo", n - 1 if e >= 1 else n)
                for h in range(HALF):
                    ins = act.activation(g32[:, e % 2, h, :], bH[:, h, :], ACT.Gelu, bias=b1[:, e, h:h + 1], scale=1.0 / WS)
                ins.then_inc(s["gelu"], 1)

            def body(it, g):
                for e in range(E):
                    if it is not None:
                        gelu(it, e)
                    for p in (2 * e, 2 * e + 1):
                        if it is not None:
                            router(it, p)
                        if g is not None:
                            attention(g, p)
                if g is not None:
                    tail(g)

            high_weights()
            body(None, 0)
            body(0, 1)
            with act.Fori(1, GROUPS - 1) as it:
                body(it, it + 1)
            body(GROUPS - 1, None)

        @block.tensor
        def _(pe):
            ones_row = cst[0:1, where["ones"][0]:where["ones"][0] + P]
            one = cst[0:1, where["ones"][0]:where["ones"][0] + 1]
            pe.wait_ge(s["ld_c"], 16)
            pe.wait_ge(s["ld_r"], 16 * 14)
            for i in range(3):
                pe.transpose(bA[:, i * P:(i + 1) * P], w_in[:, i, :], ident)
            pe.transpose(bA[:, 3 * P:3 * P + E * HALF], b1_in[:, :], ident[0:E * HALF, 0:E * HALF]).then_inc(s["i_wt"], 1)
            pe.wait_ge(s["i_rep"], 16)
            pe.matmul(bB, ones_row, rows[:, 0:4, :], start=True, stop=True)
            pe.matmul(bC[:, 0:2 * P], ones_row, rows[:, 4:6, :], start=True, stop=True)
            pe.matmul(bC[:, 2 * P:2 * P + E], ones_row, rb_row[:, :], start=True, stop=True)
            for i in range(2):
                for b in range(BLK):
                    at = 2 * P + E + BLK * i + b
                    m = pe.matmul(bC[:, at:at + 1], rep_rows[:, i, b, :, :, :], one, start=True, stop=True)
            m.then_inc(s["i_bc"], 1)

            def attention(g, p):
                if p == AT["x_t"]:
                    pe.wait_ge(s["ld_x"], 16 * (g + 1))
                    if isinstance(g, int) and g == 0:
                        pe.wait_ge(s["i_wtc"], 3)
                        pe.wait_ge(s["i_bcc"], 4)
                    since(pe, "x2l", g)
                    since(pe, "x_tc", g)
                    for b in range(B):
                        m = pe.transpose(bA[:, b * P:(b + 1) * P], x[:, b, :], ident)
                    m.then_inc(s["x_tp"], 1)
                    pe.wait_ge(s["ld_cx"], 16 * (g + 1))
                    since(pe, "y2", g)
                    for b in range(B):
                        m = pe.transpose(bB[:, b * CTX:(b + 1) * CTX], cx[:, b, :], ident[0:CTX, 0:CTX])
                    m.then_inc(s["cx_tp"], 1)
                if p == AT["proj"]:
                    since(pe, "x_tc", g + 1)
                    pe.matmul(bA, wq_t[:, :], x_t[:, :], start=True, stop=True).then_inc(s["proj"], 1)
                    since(pe, "prob", B * g)
                    for b in range(B):
                        m = pe.matmul((bC, bD)[b // 2][:, (b % 2) * 2 * P:(b % 2 + 1) * 2 * P], x_t[:, b * P:(b + 1) * P],
                                      wkv_t[:, :, :], start=True, stop=True)
                    m.then_inc(s["proj"], 1)
                    since(pe, "cx_tc", g + 1)
                    for b in range(B):
                        m = pe.matmul(bB[0:CTX, b * P:(b + 1) * P], cx_t[:, b * CTX:(b + 1) * CTX], xw[:, 2, :], start=True, stop=True)
                    m.then_inc(s["v1_p"], 1)
                if p == AT["rot"]:
                    since(pe, "q", g + 1)
                    pe.matmul(bA, c_("rot"), q[:, :], start=True, stop=True).then_inc(s["rot"], 1)
                    since(pe, "kg", g + 1)
                    since(pe, "kb", g + 1)
                    since(pe, "v", g + 1)
                    pe.wait_ge(s["i_ones"], 2)
                    for b in range(B):
                        m = pe.matmul(bD[:, b:b + 1], kg[:, b, :], mean_col[:, :], start=True, stop=True)
                    m.then_inc(s["k_mean_p"], 1)
                if p == AT["kv"]:
                    since(pe, "kr", g + 1)
                    for b in range(B):
                        m = pe.matmul(bC[:, b * P:(b + 1) * P], kr[:, b, :], v[:, b, :], start=True, stop=True)
                    m.then_inc(s["kv_p"], 1)
                if p == AT["out"]:
                    since(pe, "k_mean", g + 1)
                    for b in range(B):
                        m = pe.matmul(bD[:, 16 + b * HEADS:16 + (b + 1) * HEADS], q[:, b * P:(b + 1) * P], k_mean[:, b, :], start=True, stop=True)
                    m.then_inc(s["d_p"], 1)
                    since(pe, "kv", g + 1)
                    since(pe, "qr", g + 1)
                    for b in range(B):
                        m = pe.matmul(bA[:, b * P:(b + 1) * P], qr[:, b * P:(b + 1) * P], kv[:, b, :], start=True, stop=True)
                    m.then_inc(s["out_p"], 1)
                for first, at in ((0, "k_rep"), (2, "k_rep2")):
                    if p == AT[at]:
                        since(pe, "v1", g + 1)
                        since(pe, "kv", g + 1)
                        if first:
                            since(pe, "k_rep", 4 * g + 2)
                        for i in (first, first + 1):
                            m = pe.matmul((bB, bC)[i % 2][:, 0:B * CTX], wk_rep[:, i, :, :, :], cx_t[:, :], start=True, stop=True)
                        m.then_inc(s["k_rep_p"], 1)
                if p == AT["x1_t"]:
                    since(pe, "x1", g + 1)
                    for b in range(B):
                        m = pe.transpose(bA[:, b * P:(b + 1) * P], x1[:, b, :], ident)
                    m.then_inc(s["x1_tp"], 1)
                if p == AT["q_rep"]:
                    since(pe, "x1_tc", g + 1)
                    since(pe, "k_rep", 4 * (g + 1))
                    since(pe, "den", g + 1)
                    for i in range(BLK):
                        m = pe.matmul(ps[:, i, :], wq_rep[:, i, :, :, :], x1_t[:, :], start=True, stop=True)
                    m.then_inc(s["q_rep_p"], 1)
                for b in range(B):
                    n = B * g + b
                    at = AT["scores"] + AT["per_seq"] * b
                    if p == at:
                        if b == 0:
                            since(pe, "q_rep", 4 * (g + 1))
                        else:
                            values(g, b - 1)
                        scores(n, b)
                    if p == at + 1:
                        since(pe, "mxl", n + 1)
                        since(pe, "ao", n)
                        pe.wait_ge(s["i_idb"], 2)
                        if b == 0 and not isinstance(g, int):
                            since(pe, "acc0", g)
                        pe.transpose(ps[:, 4, 0:P // 2].bitcast(BF16), mx_hl[:, :, :, :], identb[:, :]).then_inc(s["mxt_p"], 1)
                    if p == at + 2:
                        scores_t(n, b)
                if p == AT["scores"] + AT["per_seq"] * B:
                    values(g, B - 1)
                if p == AT["ao_t"]:
                    since(pe, "ao", B * (g + 1))
                    since(pe, "prob", B * (g + 1))
                    for b in range(B):
                        m = pe.transpose(bA[:, b * P:(b + 1) * P], ao[:, b, :], ident)
                    m.then_inc(s["ao_tp"], 1)
                if p == AT["wo"]:
                    since(pe, "ao_tc", g + 1)
                    for b in range(B):
                        m = pe.matmul(bB[:, b * P:(b + 1) * P], ao_t[:, b * P:(b + 1) * P], xw[:, 3, :], start=True, stop=True)
                    m.then_inc(s["wo_p"], 1)

            def scores(n, b):
                since(pe, "prob", n)
                for i in range(BLK):
                    for r in range(4):
                        m = pe.matmul(ps[:, r, i * CTX:(i + 1) * CTX], q_rep[32 * r:32 * r + 32, i, b * P:(b + 1) * P],
                                      k_rep[32 * r:32 * r + 32, i, b * CTX:(b + 1) * CTX], start=True, stop=True)
                m.then_inc(s["s_p"], 1)

            def scores_t(n, b):
                since(pe, "mxt_c", n + 1)
                since(pe, "mx", n + 1)
                for i in range(BLK):
                    for r in range(4):
                        pe.matmul(ps[0:CTX, r, i * P:(i + 1) * P], k_rep[32 * r:32 * r + 32, i, b * CTX:(b + 1) * CTX],
                                  q_rep[32 * r:32 * r + 32, i, b * P:(b + 1) * P], start=True, stop=False)
                    for r in range(4):
                        m = pe.matmul(ps[0:CTX, r, i * P:(i + 1) * P], pick[32 * r:32 * r + 32, i, :],
                                      mx_t[32 * r:32 * r + 32, :], start=False, stop=True)
                m.then_inc(s["t_p"], 1)

            def values(g, b):
                n = B * g + b
                since(pe, "prob", n + 1)
                since(pe, "mxt_c", n + 1)
                since(pe, "v1", g + 1)
                for h in range(HEADS):
                    r, i = h % 4, h // 4
                    m = pe.matmul(bE[:, P + h * AVW:P + (h + 1) * AVW], prob[:, (4 * r + i) * P:(4 * r + i + 1) * P],
                                  v1[:, b, h, :], start=True, stop=True)
                m.then_inc(s["av_p"], 1)

            def tail(g):
                since(pe, "x2n", g + 1)
                for b in range(B):
                    m = pe.transpose(bA[:, b * P:(b + 1) * P], x2n[:, b, :], ident)
                m.then_inc(s["x2_tp"], 1)

            def router(it, p):
                if p == AT["logits"]:
                    since(pe, "x2l", it + 1)
                    pe.wait_ge(s["i_rwl"], 2)
                    since(pe, "ao", B * (it + 1))
                    for b in range(B):
                        o = bE[:, b * E:(b + 1) * E]
                        xh, xl = x2h[:, b * P:(b + 1) * P], x2l[:, b * P:(b + 1) * P]
                        pe.matmul(o, xh, rwh[:, :], start=True, stop=False)
                        pe.matmul(o, xh, rwl[:, :], start=False, stop=False)
                        pe.matmul(o, xl, rwh[:, :], start=False, stop=False)
                        m = pe.matmul(o, xl, rwl[:, :], start=False, stop=True)
                    m.then_inc(s["lg_p"], 1)
                if p == AT["c_t"]:
                    since(pe, "cw", it + 1)
                    for b in range(B):
                        m = pe.transpose(ps[0:E, 4, b * P:(b + 1) * P], cw[:, b, :], ident)
                    m.then_inc(s["cw_tp"], 1)
                if p == AT["b2"]:
                    since(pe, "cw_tc", it + 1)
                    pe.wait_ge(s["i_b1"], 16)
                    for b in range(B):
                        m = pe.matmul(bE[:, b * P:(b + 1) * P], cw_t[:, b * P:(b + 1) * P], b2[:, :], start=True, stop=True)
                    m.then_inc(s["b2_p"], 1)

            def first(it, e):
                n = E * it + e
                if e == 0:
                    since(pe, "x2l", it + 1)
                since(pe, "gelu", n)
                for h in range(HALF):
                    wh, wl = w1h[:, e, h * P:(h + 1) * P], w1l[:, e, h * P:(h + 1) * P]
                    pe.matmul(bH[:, h, :], wh, x2h[:, :], start=True, stop=False)
                    pe.matmul(bH[:, h, :], wh, x2l[:, :], start=False, stop=False)
                    m = pe.matmul(bH[:, h, :], wl, x2h[:, :], start=False, stop=True)
                m.then_inc(s["h_p"], 1)

            def second(it, e):
                n = E * it + e
                since(pe, "lo", n + 1)
                since(pe, "comb", n)
                for b in range(B):
                    for h in range(HALF):
                        o = bY[:, b * P:(b + 1) * P]
                        ghb, glb = gh[:, e % RING, h, b * P:(b + 1) * P], gl[:, e % RING, h, b * P:(b + 1) * P]
                        pe.matmul(o, ghb, w2h[:, e, h, :], start=(h == 0), stop=False)
                        pe.matmul(o, ghb, w2l[:, e, h, :], start=False, stop=False)
                        m = pe.matmul(o, glb, w2h[:, e, h, :], start=False, stop=(h == HALF - 1))
                m.then_inc(s["y_p"], 1)

            def body(it, g):
                for e in range(E):
                    if it is not None:
                        first(it, e)
                    for p in (2 * e, 2 * e + 1):
                        if it is not None:
                            router(it, p)
                        if g is not None:
                            attention(g, p)
                        if it is not None and p % 2 == 0 and e >= LAG:
                            second(it, e - LAG)
                if it is not None:
                    for e in range(E - LAG, E):
                        second(it, e)
                if g is not None:
                    tail(g)

            body(None, 0)
            pe.wait_ge(s["i_w1"], 1)
            pe.wait_ge(s["i_w2"], 1)
            body(0, 1)
            with pe.Fori(1, GROUPS - 1) as it:
                body(it, it + 1)
            body(GROUPS - 1, None)

        @block.vector
        def _(dve):
            dve.wait_ge(s["i_rwl"], 1)
            dve.scalar_tensor_tensor(out=rwl[:, :], in0=rw[:, :], scalar=WS, in1=rwh[:, :], op0=ALU.mult, op1=ALU.subtract).then_inc(s["i_rwl"], 1)
            dve.wait_ge(s["i_bcc"], 4)
            dve.tensor_scalar(b_neg[:, 0, :], b_rep[:, 0, :], c_("q_low"), None, ALU.mult).then_inc(s["i_bn"], 1)
            dve.tensor_scalar(b_neg[:, 1, :], b_rep[:, 1, :], c_("k_low"), None, ALU.mult).then_inc(s["i_bn"], 1)
            dve.wait_ge(s["i_w1h"], 1)
            dve.scalar_tensor_tensor(out=w1l[:, :, :].rearrange("p e n -> p (e n)"), in0=w_stage[:, :], scalar=WS,
                                     in1=w1h[:, :, :].rearrange("p e n -> p (e n)"), op0=ALU.mult, op1=ALU.subtract).then_inc(s["i_w1"], 1)
            dve.wait_ge(s["i_w2h"], 1)
            dve.scalar_tensor_tensor(out=w2l[:, :, :, :].rearrange("p e h n -> p (e h n)"), in0=w_stage[:, :], scalar=WS,
                                     in1=w2h[:, :, :, :].rearrange("p e h n -> p (e h n)"), op0=ALU.mult, op1=ALU.subtract).then_inc(s["i_w2"], 1)

            def static_wait():
                dve.wait_ge(s["i_bcc"], 4)

            def moments(k, src, g, st, ag, vn, eps):
                since(dve, ("x1", "x1", "x2n", "fin")[k] if k else "y1", g)
                for b in range(B):
                    m = dve.bn_stats(stats[:, k, b, :], src[:, b, :])
                m.then_inc(s[st], 1)
                static_wait()
                since(dve, st, g + 1)
                for b in range(B):
                    m = dve.bn_aggr(mv[:, k, b, :], stats[:, k, b, :])
                m.then_inc(s[ag], 1)
                since(dve, ag, g + 1)
                dve.tensor_scalar(ve[:, k, :], mv[:, k, :, 1], eps, None, ALU.add).then_inc(s[vn], 1)

            def attention(g, p):
                if p == AT["proj"]:
                    since(dve, "proj", 2 * (g + 1))
                    since(dve, "kg", g)
                    since(dve, "i_bcc", 4)
                    for j in range(2):
                        m = dve.tensor_tensor(kb[:, 2 * j:2 * j + 2, :], ps[:, 2 + j, :].rearrange("p (b i n) -> p b i n", b=2, i=2)[:, :, 0, :],
                                              wide[:, 0:1, :].broadcast_to([P, 2, P]), ALU.add)
                    m.then_inc(s["kb"], 1)
                    since(dve, "kv_p", g)
                    for j in range(2):
                        m = dve.tensor_tensor(v[:, 2 * j:2 * j + 2, :], ps[:, 2 + j, :].rearrange("p (b i n) -> p b i n", b=2, i=2)[:, :, 1, :],
                                              wide[:, 1:2, :].broadcast_to([P, 2, P]), ALU.add)
                    m.then_inc(s["v"], 1)
                    since(dve, "qg", g + 1)
                    since(dve, "rot", g)
                    since(dve, "d_p", g)
                    dve.tensor_scalar(q[:, :], qg[:, :], 0.21, None, ALU.add).then_inc(s["q"], 1)
                if p == AT["proj"] + 1:
                    since(dve, "kg", g + 1)
                    since(dve, "kr", g)
                    dve.scalar_tensor_tensor(out=k_cos[:, :, :], in0=kg[:, :, :], scalar=0.21, in1=wide_b(c_("cos")), op0=ALU.add, op1=ALU.mult).then_inc(s["k_cos"], 1)
                    for to, name in ((0, "sin_neg"), (1, "sin")):
                        dve.scalar_tensor_tensor(out=k_sin[:, :, to::2], in0=kg[:, :, 1 - to::2], scalar=0.21, in1=wide_b(c_(name)),
                                                 op0=ALU.add, op1=ALU.mult).then_inc(s["k_sin"], 1)
                    since(dve, "q", g + 1)
                    since(dve, "qr", g)
                    dve.tensor_tensor(by_seq(q_cos), by_seq(q), wide_b(c_("cos_t")), ALU.mult).then_inc(s["q_cos"], 1)
                    since(dve, "v1_p", g + 1)
                    since(dve, "av_p", B * g)
                    pool_ones()
                    for b in range(B):
                        m = dve.tensor_tensor(v1[:, b, :, 0:HD], bB[0:CTX, b * P:(b + 1) * P].rearrange("p (h d) -> p h d", d=HD),
                                              wide[0:CTX, 4, :].rearrange("p (h d) -> p h d", d=HD), ALU.add)
                    m.then_inc(s["v1"], 1)
                if p == AT["rot"]:
                    since(dve, "rot", g + 1)
                    dve.tensor_tensor(by_seq(q_sin), by_seq(bA), wide_b(c_("sin_t")), ALU.mult).then_inc(s["q_sin"], 1)
                    since(dve, "k_mean_p", g + 1)
                    since(dve, "d_p", g)
                    dve.scalar_tensor_tensor(out=k_mean[:, :, :], in0=bD[:, 0:B].rearrange("p (b a) -> p b a", a=1).broadcast_to([P, B, HEADS]),
                                             scalar=0.21, in1=c_("head_of").rearrange("p (a h) -> p a h", a=1).broadcast_to([P, B, HEADS]),
                                             op0=ALU.add, op1=ALU.mult).then_inc(s["k_mean"], 1)
                if p == AT["kv"]:
                    since(dve, "kv_p", g + 1)
                    since(dve, "out_p", g)
                    dve.tensor_tensor(kv[:, :, :], by_seq(bC), wide_b(c_("same_head")), ALU.mult).then_inc(s["kv"], 1)
                if p == AT["out"]:
                    since(dve, "d_p", g + 1)
                    dve.tensor_scalar(den[:, :], bD[:, 16:16 + B * HEADS], 1e-6, None, ALU.add).then_inc(s["den"], 1)
                    since(dve, "den", g + 1)
                    since(dve, "oz", g)
                    dve.reciprocal(z[:, :], den[:, :]).then_inc(s["z"], 1)
                    since(dve, "out_p", g + 1)
                    since(dve, "z", g + 1)
                    since(dve, "res", g)
                    dve.tensor_tensor(oz[:, :, :].rearrange("p b (h d) -> p (b h) d", d=HD), bA.rearrange("p (n d) -> p n d", d=HD),
                                      z[:, :].rearrange("p (n a) -> p n a", a=1).broadcast_to([P, B * HEADS, HD]), ALU.mult).then_inc(s["oz"], 1)
                for at, first in (("k_rep", 0), ("k_rep2", 2)):
                    if p == AT[at]:
                        since(dve, "s_p", B * g)
                        since(dve, "t_p", B * g)
                        for i in (first, first + 1):
                            since(dve, "k_neg", 4 * g + i + 1)
                            dve.scalar_tensor_tensor(out=k_rep[:, i, :], in0=(bB, bC)[i % 2][:, 0:B * CTX], scalar=b_rep[:, 1, i:i + 1],
                                                     in1=k_neg[:, i, :], op0=ALU.add, op1=ALU.add).then_inc(s["k_rep"], 1)
                if p == AT["out"] + 1:
                    since(dve, "res", g + 1)
                    moments(0, res, g, "st1", "ag1", "ve1", 1e-12)
                    since(dve, "y1", g)
                    for b in range(B):
                        m = dve.scalar_tensor_tensor(out=resg[:, b, :], in0=res[:, b, :], scalar=mv[:, 0, b, 0:1], in1=wide[:, 2, :],
                                                     op0=ALU.subtract, op1=ALU.mult)
                    m.then_inc(s["resg"], 1)
                if p == AT["out"] + 2:
                    since(dve, "rs1", g + 1)
                    since(dve, "resg", g + 1)
                    since(dve, "x_beta", g + 1)
                    for b in range(B):
                        m = dve.scalar_tensor_tensor(out=y1[:, b, :], in0=resg[:, b, :], scalar=rstd[:, 0, b:b + 1], in1=x_beta[:, b, :],
                                                     op0=ALU.mult, op1=ALU.add)
                    m.then_inc(s["y1"], 1)
                    since(dve, "y1", g + 1)
                    moments(1, y1, g, "st2", "ag2", "ve2", 1e-5)
                if p == AT["out"] + 3:
                    since(dve, "rs2", g + 1)
                    since(dve, "x1_bo", g)
                    since(dve, "x1_tp", g)
                    for b in range(B):
                        m = dve.tensor_scalar(x1[:, b, :], y1[:, b, :], mv[:, 1, b, 0:1], rstd[:, 1, b:b + 1], ALU.subtract, ALU.mult)
                    m.then_inc(s["x1"], 1)
                if p == AT["q_rep"]:
                    since(dve, "t_p", B * g)
                    for i in range(BLK):
                        since(dve, "q_neg", 4 * g + i + 1)
                        dve.scalar_tensor_tensor(out=q_rep[:, i, :], in0=ps[:, i, :], scalar=b_rep[:, 0, i:i + 1],
                                                 in1=q_neg[:, i, :], op0=ALU.add, op1=ALU.add).then_inc(s["q_rep"], 1)
                for b in range(B):
                    n = B * g + b
                    at = AT["scores"] + AT["per_seq"] * b
                    if p == at:
                        since(dve, "s_p", n + 1)
                        since(dve, "mxl", n)
                        dve.tensor_reduce(mx[:, :, :], ps[:, 0:4, 0:BLK * CTX].rearrange("p r (i k) -> p r i k", i=BLK), AX.X, ALU.max).then_inc(s["mx"], 1)
                        since(dve, "mx", n + 1)
                        since(dve, "mxt_p", n)
                        mxb = mx[:, :, :].rearrange("p (a r) i -> p a (r i)", a=1).broadcast_to([P, 4, HEADS])
                        dve.tensor_copy(mx_hl[:, :, 0, :], mxb).then_inc(s["mxh"], 1)
                        since(dve, "mxh", n + 1)
                        dve.tensor_tensor(mx_hl[:, :, 1, :], mxb, mx_hl[:, :, 0, :], ALU.subtract).then_inc(s["mxl"], 1)
                    if p == at + 3:
                        since(dve, "av_p", n + 1)
                        since(dve, "ao", n)
                        av = bE[:, P:P + HEADS * AVW].rearrange("p (h d) -> p h d", d=AVW)
                        dve.reciprocal(rs[:, :], av[:, :, HD]).then_inc(s["rs_"], 1)
                        since(dve, "rs_", n + 1)
                        since(dve, "ao_tp", g)
                        dve.tensor_tensor(ao[:, b, :].rearrange("p (h d) -> p h d", d=HD), av[:, :, 0:HD],
                                          rs[:, :].rearrange("p (h a) -> p h a", a=1).broadcast_to([P, HEADS, HD]), ALU.mult).then_inc(s["ao"], 1)
                if p == AT["wo"]:
                    since(dve, "wo_p", g + 1)
                    since(dve, "x1_bo", g + 1)
                    since(dve, "x2n", g)
                    dve.tensor_tensor(y2[:, :, :], by_seq(bB), x1_bo[:, :, :], ALU.add).then_inc(s["y2"], 1)
                    since(dve, "y2", g + 1)
                    moments(2, y2, g, "st3", "ag3", "ve3", 1e-5)
                if p == AT["wo"] + 1:
                    since(dve, "rs3", g + 1)
                    since(dve, "x2_tp", g)
                    since(dve, "acc0", g)
                    for b in range(B):
                        m = dve.tensor_scalar(x2n[:, b, :], y2[:, b, :], mv[:, 2, b, 0:1], rstd[:, 2, b:b + 1], ALU.subtract, ALU.mult)
                    m.then_inc(s["x2n"], 1)

            def pool_ones():
                dve.wait_ge(s["i_v1"], 1)

            def wide_b(ap):
                return ap.rearrange("p (a n) -> p a n", a=1).broadcast_to([P, B, ap.shape[1]])

            def by_seq(ap):
                return ap[:, :].rearrange("p (b n) -> p b n", b=B)

            def tail(g):
                since(dve, "x2h", g + 1)
                since(dve, "h_p", E * g)
                since(dve, "lg_p", g)
                dve.tensor_tensor(x2l[:, :], bA, x2h[:, :], ALU.subtract).then_inc(s["x2l"], 1)

            def router(it, p):
                if p == AT["logits"]:
                    since(dve, "lg_p", it + 1)
                    dve.wait_ge(s["i_lg"], 1)
                    since(dve, "chosen", it)
                    since(dve, "lgm", it)
                    dve.scalar_tensor_tensor(out=lg[:, :, 0:E], in0=bE[:, 0:B * E].rearrange("p (b e) -> p b e", b=B), scalar=1.0 / WS,
                                             in1=wide_b(rb[:, :]), op0=ALU.mult, op1=ALU.add).then_inc(s["lg"], 1)
                    static_wait()
                    since(dve, "lg", it + 1)
                    since(dve, "cut", it)
                    for b in range(B):
                        m = dve.max(top[:, b, :], lg[:, b, :])
                    m.then_inc(s["top"], 1)
                    since(dve, "top", it + 1)
                    since(dve, "th", it)
                    dve.tensor_tensor(lgm[:, :, :], lg[:, :, 0:E], top[:, :, 0:1].broadcast_to([P, B, E]), ALU.subtract).then_inc(s["lgm"], 1)
                    since(dve, "lgm", it + 1)
                    dve.memset(top[:, :, TOPK:8], FAR).then_inc(s["topx"], 1)
                    static_wait()
                    since(dve, "topx", it + 1)
                    for b in range(B):
                        m = dve.match_replace(cut[:, b, :], top[:, b, :], lg[:, b, :], -FAR)
                    m.then_inc(s["cut"], 1)
                    since(dve, "cut", it + 1)
                    since(dve, "pm", it)
                    dve.tensor_tensor(chosen[:, :, :], cut[:, :, 0:E], lg[:, :, 0:E], ALU.not_equal).then_inc(s["chosen"], 1)
                if p == AT["logits"] + 2:
                    since(dve, "th", it + 1)
                    dve.tensor_scalar(dnm[:, :, :], th[:, :, :], -1.0, 1.0, ALU.mult, ALU.add).then_inc(s["dnm"], 1)
                    since(dve, "chosen", it + 1)
                    dve.scalar_tensor_tensor(out=num[:, :, :], in0=th[:, :, :], scalar=1.0, in1=chosen[:, :, :], op0=ALU.add, op1=ALU.mult).then_inc(s["num"], 1)
                    since(dve, "dnm", it + 1)
                    dve.reciprocal(rdn[:, :, :], dnm[:, :, :]).then_inc(s["rdn"], 1)
                    since(dve, "rdn", it + 1)
                    since(dve, "num", it + 1)
                    dve.tensor_tensor(pm[:, :, :], num[:, :, :], rdn[:, :, :], ALU.mult).then_inc(s["pm"], 1)
                    since(dve, "pm", it + 1)
                    dve.tensor_reduce(ps_[:, :], pm[:, :, :], AX.X, ALU.add).then_inc(s["ps_"], 1)
                    since(dve, "ps_", it + 1)
                    dve.tensor_scalar(ps2[:, :], ps_[:, :], WS, None, ALU.mult).then_inc(s["ps2"], 1)
                    since(dve, "ps2", it + 1)
                    dve.reciprocal(rps[:, :], ps2[:, :]).then_inc(s["rps"], 1)
                    since(dve, "rps", it + 1)
                    since(dve, "comb", E * it)
                    since(dve, "cw_tp", it)
                    dve.tensor_tensor(cw[:, :, :], pm[:, :, :], rps[:, :].rearrange("p (b a) -> p b a", a=1).broadcast_to([P, B, E]), ALU.mult).then_inc(s["cw"], 1)
                if p == AT["b2"]:
                    since(dve, "b2_p", it + 1)
                    since(dve, "fin", it)
                    dve.scalar_tensor_tensor(out=acc[:, :, :], in0=by_seq(bE), scalar=WS, in1=x2n[:, :, :], op0=ALU.mult, op1=ALU.add).then_inc(s["acc0"], 1)

            def high(it, e):
                n = E * it + e
                since(dve, "gelu", n + 1)
                since(dve, "y_p", n - RING + 1 if e >= RING - 1 else E * it)
                dve.tensor_copy(gh[:, e % RING, :, :], g32[:, e % 2, :, :]).then_inc(s["hi"], 1)

            def combine(it, e):
                n = E * it + e
                since(dve, "y_p", n + 1)
                if e == 0:
                    since(dve, "acc0", it + 1)
                    since(dve, "cw", it + 1)
                since(dve, "comb", n)
                for b in range(B):
                    m = dve.scalar_tensor_tensor(out=acc[:, b, :], in0=bY[:, b * P:(b + 1) * P], scalar=cw[:, b, e:e + 1], in1=acc[:, b, :],
                                                 op0=ALU.mult, op1=ALU.add)
                m.then_inc(s["comb"], 1)

            def finish(it):
                since(dve, "comb", E * (it + 1))
                moments(3, acc, it, "st4", "ag4", "ve4", 1e-5)
                since(dve, "rs4", it + 1)
                since(dve, "st_out", 16 * it)
                for b in range(B):
                    m = dve.tensor_scalar(fin[:, b, :], acc[:, b, :], mv[:, 3, b, 0:1], rstd[:, 3, b:b + 1], ALU.subtract, ALU.mult)
                m.then_inc(s["fin"], 1)

            def body(it, g):
                for e in range(E):
                    if it is not None:
                        high(it, e)
                    for p in (2 * e, 2 * e + 1):
                        if it is not None:
                            router(it, p)
                        if g is not None:
                            attention(g, p)
                        if it is not None and p % 2 == 0 and e >= LAG:
                            combine(it, e - LAG)
                if it is not None:
                    for e in range(E - LAG, E):
                        combine(it, e)
                    finish(it)
                if g is not None:
                    tail(g)

            body(None, 0)
            body(0, 1)
            with dve.Fori(1, GROUPS - 1) as it:
                body(it, it + 1)
            body(GROUPS - 1, None)


_INS = ['x', 'ctx_1024', 'L0_attn_Wq', 'L0_attn_bq', 'L0_attn_Wk', 'L0_attn_bk', 'L0_attn_Wv', 'L0_attn_bv', 'L0_attn_gamma',
        'L0_attn_beta', 'L0_xattn_Wq', 'L0_xattn_bq', 'L0_xattn_Wk', 'L0_xattn_bk', 'L0_xattn_Wv', 'L0_xattn_bv', 'L0_xattn_Wo',
        'L0_xattn_bo', 'L0_ffn_router_w', 'L0_ffn_router_b', 'L0_ffn_w1', 'L0_ffn_b1', 'L0_ffn_w2', 'L0_ffn_b2']


def kernel(**inputs):
    import numpy as _np
    import concourse.bacc as _bacc
    from concourse import mybir as _mybir
    from concourse.bass_utils import run_bass_kernel_spmd as _run

    nc = _bacc.Bacc("TRN2", target_bir_lowering=False, num_devices=1)
    arrays, aps = {}, {}
    for name in _INS:
        a = _np.ascontiguousarray(inputs[name])
        arrays[f"in_{name}"] = a
        aps[name] = nc.dram_tensor(f"in_{name}", a.shape, _mybir.dt.from_np(a.dtype), kind="ExternalInput").ap()
    table, where = constants()
    arrays["constants"] = table
    consts = nc.dram_tensor("constants", table.shape, F32, kind="ExternalInput").ap()
    out = nc.dram_tensor("out", (SEQS, P, P), F32, kind="ExternalOutput").ap()
    build(nc, aps, consts, where, out)
    r = _run(nc, [arrays], core_ids=[0])
    return r.results[0]["out"]
```

```python
from contextlib import ExitStack

import numpy as np
import concourse.bass as bass
from concourse import mybir

ALU = mybir.AluOpType
ACT = mybir.ActivationFunctionType
AX = mybir.AxisListType
F32 = mybir.dt.float32
F16 = mybir.dt.float16
BF16 = mybir.dt.bfloat16

P = 128
B = 4
SEQS = 32
GROUPS = SEQS // B
T = B * P
CTX = 77
HEADS = 16
HD = 8
BLK = 4
E = 16
HID = 256
HALF = HID // P
TOPK = 4
LAG = 3
RING = 4
WS = 256.0
FAR = -3.0e38
THETA = 10000.0


def constants():
    half = np.arange(0, P, 2, dtype=np.float32)
    inv = (np.float32(1.0) / np.float32(THETA) ** (half / np.float32(P))).astype(np.float32)
    ang = (np.arange(P, dtype=np.float32)[:, None] * inv).astype(np.float32)
    cos, sin = np.cos(ang).astype(np.float32), np.sin(ang).astype(np.float32)
    cos2, sin2 = np.repeat(cos, 2, axis=1), np.repeat(sin, 2, axis=1)
    ident = np.eye(P, dtype=np.float32)
    rot = np.zeros((P, P), np.float32)
    for i in range(0, P, 2):
        rot[i + 1, i] = -1.0
        rot[i, i + 1] = 1.0
    ch = np.arange(P)
    same_head = (ch[:, None] // HD == ch[None, :] // HD).astype(np.float32) / P
    head_of = (ch[:, None] // HD == np.arange(HEADS)[None, :]).astype(np.float32)
    pick = np.zeros((P, BLK, CTX), np.float32)
    for r in range(4):
        for hl in range(2):
            for b in range(BLK):
                pick[32 * r + 16 * hl + 4 * r + b, b] = -1.0
    cols = dict(ident=ident, rot=rot, cos=cos2, sin_neg=-sin, sin=sin, cos_t=cos2.T, sin_t=sin2.T,
                same_head=same_head, head_of=head_of,
                pick=pick.reshape(P, BLK * CTX))
    at, where = 0, {}
    for k, v in cols.items():
        where[k] = (at, v.shape[1])
        at += v.shape[1]
    return np.ascontiguousarray(np.concatenate(list(cols.values()), axis=1), np.float32), where


AT = dict(x_t=0, q=1, kv01=3, kv23=5, rot=7, k_mean=9, kv=11, den=13, out=15, norm1=17, norm2=19, x1=21,
          cx_t=0, v1=1, k=3, k_rep=5, q_rep=7, ao_t=27, wo=28,
          logits=0, weights=2, c_t=16, b2=17, acc_b2=18)
SCORES = (8, 9, 10, 11)
MAX_T = 13
SCORES_T = (14, 16, 19, 22)
VALUES = (19, 21, 23, 25)
HIGH_W = (6, 7, 8, 9, 41, 42, 43, 44)
LOW_W = (9, 10, 11, 12, 41, 42, 43, 44)
POOL_COLS = 3 * B * P


def build(nc, A, consts, where, out):
    ctx = ExitStack()
    with ctx:
        def sb(name, shape, dt=F32):
            return ctx.enter_context(nc.sbuf_tensor(name, shape, dt))

        def sem(name):
            return ctx.enter_context(nc.semaphore(name))

        cst = sb("cst", [P, consts.shape[1]])

        def c_(name):
            a, n = where[name]
            return cst[:, a:a + n]

        ident = c_("ident")
        identb = sb("identb", [P, P], BF16)
        pick = sb("pick", [P, BLK, CTX], BF16)
        mean_col = sb("mean_col", [P, 1])
        half_pow = sb("half_pow", [P, B])
        w_in = sb("w_in", [P, 3, P])
        wq_t = sb("wq_t", [P, P])
        wkv_t = sb("wkv_t", [P, 2, P])
        xw = sb("xw", [P, 4, P])
        rep4 = sb("rep4", [P, 2, 2, BLK, 4, 4, HD], F16)
        wide = sb("wide", [P, 6, P])
        rb = sb("rb", [P, E])
        bq = sb("bq", [P, 1])
        xbq = sb("xbq", [P, 1])
        xbk = sb("xbk", [P, 1])
        rw = sb("rw", [P, E])
        rwh = sb("rwh", [P, E], F16)
        rwl = sb("rwl", [P, E], F16)
        b1_in = sb("b1_in", [E * HALF, P])
        b1 = sb("b1", [P, E, HALF])
        b2 = sb("b2", [E, P])
        w_stage = sb("w_stage", [P, E * HID])
        w1h = sb("w1h", [P, E, HID], F16)
        w1l = sb("w1l", [P, E, HID], F16)
        w2h = sb("w2h", [P, E, HALF, P], F16)
        w2l = sb("w2l", [P, E, HALF, P], F16)
        x = sb("x", [P, B, P])
        cx = sb("cx", [CTX, B, P])
        x_t = sb("x_t", [P, T])
        cx_t = sb("cx_t", [P, B * CTX])
        qg = sb("qg", [P, T])
        q = sb("q", [P, T])
        q_cos = sb("q_cos", [P, T])
        q_sin = sb("q_sin", [P, T])
        qr = sb("qr", [P, T])
        kb = sb("kb", [P, B, P])
        v = sb("v", [P, B, P])
        kg = sb("kg", [P, B, P])
        k_cos = sb("k_cos", [P, B, P])
        k_sin = sb("k_sin", [P, B, P])
        kr = sb("kr", [P, B, P])
        k_mean = sb("k_mean", [P, B, HEADS])
        kv = sb("kv", [P, B, P])
        den = sb("den", [P, B * HEADS])
        z = sb("z", [P, B * HEADS])
        oz = sb("oz", [P, B, P])
        res = sb("res", [P, B, P])
        x_beta = sb("x_beta", [P, B, P])
        resg = sb("resg", [P, B, P])
        y1 = sb("y1", [P, B, P])
        x1 = sb("x1", [P, B, P])
        x1_bo = sb("x1_bo", [P, B, P])
        x1_t = sb("x1_t", [P, T])
        v1 = sb("v1", [CTX, B, HEADS, HD])
        v_hl = sb("v_hl", [CTX, B, HEADS, 2, HD + 1], F16)
        kx = sb("kx", [P, 2, B * CTX], F16)
        qx = sb("qx", [P, 2, T], F16)
        k_rep = sb("k_rep", [P, BLK, B * CTX], F16)
        q_rep = sb("q_rep", [P, BLK, T], F16)
        mx = sb("mx", [P, B, HEADS])
        mx_hl = sb("mx_hl", [P, B, 4, 2, HEADS], BF16)
        mx_t = sb("mx_t", [P, B * P], BF16)
        prob = sb("prob", [CTX, HEADS * P])
        prob_h = sb("prob_h", [CTX, 2, HEADS * P], F16)
        prob_l = sb("prob_l", [CTX, 2, HEADS * P], F16)
        av = sb("av", [P, HEADS, HD + 1])
        rs = sb("rs", [P, HEADS])
        ao = sb("ao", [P, B, P])
        ao_t = sb("ao_t", [P, T])
        y2 = sb("y2", [P, B, P])
        x2n = sb("x2n", [P, B, P])
        stats = sb("stats", [P, 4, B, 6])
        mv = sb("mv", [P, 4, B, 2])
        ve = sb("ve", [P, 4, B])
        rstd = sb("rstd", [P, 4, B])
        x2h = sb("x2h", [P, T], F16)
        x2l = sb("x2l", [P, T], F16)
        x2 = sb("x2", [P, B, P])
        lg = sb("lg", [P, B, E + 8])
        top = sb("top", [P, B, 8])
        cut = sb("cut", [P, B, E + 8])
        chosen = sb("chosen", [P, B, E])
        lgm = sb("lgm", [P, B, E])
        th = sb("th", [P, B, E])
        num = sb("num", [P, B, E])
        dnm = sb("dnm", [P, B, E])
        rdn = sb("rdn", [P, B, E])
        pe_ = sb("pe_", [P, B, E])
        pm = sb("pm", [P, B, E])
        ps_ = sb("ps_", [P, B])
        ps2 = sb("ps2", [P, B])
        rps = sb("rps", [P, B])
        cw = sb("cw", [P, B, E])
        cw_t = sb("cw_t", [E, T])
        acc = sb("acc", [P, B, P])
        acc_all = sb("acc_all", [P, B, P])
        g32 = sb("g32", [P, 2, HALF, T])
        ghl = sb("ghl", [P, 2, RING, HALF, T], F16)
        gh, gl = ghl[:, 0], ghl[:, 1]
        stages = [w_stage[:, :], ghl[:, :, :, :, :].rearrange("p i r h t -> p (i r h t)").bitcast(F32)]
        w_high = [w1h[:, :, :].rearrange("p e n -> p (e n)"), w2h[:, :, :, :].rearrange("p e h n -> p (e h n)")]
        w_low = [w1l[:, :, :].rearrange("p e n -> p (e n)"), w2l[:, :, :, :].rearrange("p e h n -> p (e h n)")]
        fin = sb("fin", [P, B, P])

        ps = ctx.enter_context(nc.psum_tensor("ps", [P, 8, 512], F32))
        bA, bB, bC, bD, bE, bY = (ps[:, i, :] for i in range(6))
        bH = ps[:, 6:8, :]

        names = """ld_c ld_wide ld_xwide ld_xw ld_b ld_in ld_w1 ld_w2 ld_x ld_cx st_out
            i_ones i_zero i_idb i_rep i_wt i_wtc i_b2 i_wh i_ws i_wl i_rw i_rwl i_v1 i_lg
            x_tp x_tc q_p qg q q_cos q_sin qr kv01_p kv23_p kb v kg k_cos k_sin kr rot_p
            k_mean_p k_mean kv_p kv d_p den z out_p oz res x_beta
            st1 ag1 ve1 rs1 resg y1 st2 ag2 ve2 rs2 x1
            cx_tp cx_tc v1_p v1 vh vl x1_bo x1_tp x1_tc k_p kxh kxl q_xp qxh qxl k_rep_p k_rep q_rep_p q_rep
            s_p mx mxh mxl mxt_p mxt_c t_p prob prob_h prob_l av_p av rs_ ao
            ao_tp ao_tc wo_p y2 st3 ag3 ve3 rs3 x2n x2_tp x2h x2l
            lg_p lg top topx cut chosen lgm th num dnm rdn pm ps_ ps2 rps cw cw_tp cw_tc b2_p acc_b2
            h_p gelu hi lo y_p comb st4 ag4 ve4 rs4 fin""".split()
        s = {n: sem("s_" + n) for n in names}

        def since(eng, name, n):
            if not (isinstance(n, int) and n <= 0):
                eng.wait_ge(s[name], n)

        def first_group(f):
            return isinstance(f, int) and f == 0

        def min_groups(n):
            return min(n, GROUPS) if isinstance(n, int) else n

        x_dram = A["x"].rearrange("(g b) n c -> g n b c", b=B)
        cx_dram = A["ctx_1024"].rearrange("(g b) n c -> g n b c", b=B)
        out_dram = out.rearrange("(g b) n c -> g n b c", b=B)

        def row(name):
            return A[name].rearrange("(a n) -> a n", a=1)

        block = ctx.enter_context(nc.Block())

        @block.sync
        def _(sp):
            def load_x(a):
                since(sp, "res", a)
                since(sp, "x_beta", a)
                sp.dma_start(x[:, :, :], x_dram[a]).then_inc(s["ld_x"], 16)

            def load_cx(a):
                since(sp, "cx_tp", a)
                sp.dma_start(cx[:, :, :], cx_dram[a]).then_inc(s["ld_cx"], 16)

            def store(f):
                since(sp, "fin", f + 1)
                sp.dma_start(out_dram[f], fin[:, :, :]).then_inc(s["st_out"], 16)

            load_x(0)
            for i, n in enumerate(("L0_attn_bk", "L0_attn_bv", "L0_attn_gamma", "L0_attn_beta")):
                sp.dma_start(wide[:, i, :], row(n).broadcast_to([P, P])).then_inc(s["ld_wide"], 16)
            load_cx(0)
            sp.dma_start(stages[0].rearrange("p (e n) -> p e n", e=E),
                         A["L0_ffn_w1"].rearrange("e c n -> c e n")).then_inc(s["ld_w1"], 16)
            sp.dma_start(stages[1].rearrange("p (e h n) -> p e h n", e=E, h=HALF),
                         A["L0_ffn_w2"].rearrange("e (h i) n -> i e h n", h=HALF)).then_inc(s["ld_w2"], 16)
            load_x(1)
            load_cx(1)
            load_x(2)
            with sp.Fori(2, GROUPS - 1) as g:
                load_cx(g)
                load_x(g + 1)
                store(g - 2)
            load_cx(GROUPS - 1)
            for g in range(GROUPS - 3, GROUPS):
                store(g)
            sp.wait_ge(s["st_out"], 16 * GROUPS)

        @block.gpsimd
        def _(pool):
            for i, n in enumerate(("L0_xattn_bv", "L0_xattn_bo")):
                pool.dma_start(wide[:, 4 + i, :], row(n).broadcast_to([P, P])).then_inc(s["ld_xwide"], 16)
            pool.dma_start(rb[:, :], row("L0_ffn_router_b").broadcast_to([P, E])).then_inc(s["ld_xwide"], 16)
            for i, n in enumerate(("L0_xattn_Wq", "L0_xattn_Wk", "L0_xattn_Wv", "L0_xattn_Wo")):
                pool.dma_start(xw[:, i, :], A[n]).then_inc(s["ld_xw"], 16)
            pool.dma_start(b2[:, :], A["L0_ffn_b2"]).then_inc(s["i_b2"], 16)
            pool.dma_start(rw[:, :], A["L0_ffn_router_w"]).then_inc(s["i_rw"], 16)
            pool.memset(rep4[:, :, :, :, :, :, :], 0.0).then_inc(s["i_zero"], 1)
            pool.memset(mean_col[:, :], 1.0 / P).then_inc(s["i_ones"], 1)
            pool.memset(half_pow[:, :], -0.5).then_inc(s["i_ones"], 1)
            pool.memset(v_hl[:, :, :, 0, HD:HD + 1], 1.0).then_inc(s["i_v1"], 1)
            pool.memset(v_hl[:, :, :, 1, HD:HD + 1], 0.0).then_inc(s["i_v1"], 1)
            pool.memset(lg[:, :, E:E + 8], FAR).then_inc(s["i_lg"], 1)
            pool.wait_ge(s["ld_c"], 16)
            pool.tensor_copy(identb[:, :], ident).then_inc(s["i_idb"], 1)
            pool.tensor_copy(pick[:, :, :], c_("pick").rearrange("p (b k) -> p b k", b=BLK)).then_inc(s["i_idb"], 1)
            pool.wait_ge(s["i_zero"], 1)
            for i, low_sets in enumerate(((2, 3), (1, 3))):
                for n in range(4):
                    pool.tensor_copy(rep4[:, i, int(n in low_sets), :, :, n, :],
                                     ident.rearrange("p (b r d) -> p b r d", b=BLK, r=4)).then_inc(s["i_rep"], 1)

            def power(n, g, name_ve, name_rs):
                since(pool, name_ve, g + 1)
                pool.tensor_tensor(rstd[:, n, :], ve[:, n, :], half_pow[:, :], ALU.pow).then_inc(s[name_rs], 1)

            def linear(a, p):
                if p == AT["q"]:
                    pool.wait_ge(s["ld_x"], 16 * (a + 1))
                    pool.wait_ge(s["ld_wide"], 16 * 4)
                    since(pool, "y1", a)
                    pool.tensor_tensor(x_beta[:, :, :], x[:, :, :], wide[:, 3:4, :].broadcast_to([P, B, P]), ALU.add).then_inc(s["x_beta"], 1)
                if p == AT["rot"]:
                    since(pool, "k_sin", 2 * (a + 1))
                    since(pool, "k_cos", a + 1)
                    since(pool, "kv_p", a)
                    pool.tensor_tensor(kr[:, :, :], k_cos[:, :, :], k_sin[:, :, :], ALU.add).then_inc(s["kr"], 1)
                if p == AT["rot"] + 1:
                    since(pool, "q_cos", a + 1)
                    since(pool, "q_sin", a + 1)
                    since(pool, "out_p", a)
                    pool.tensor_tensor(qr[:, :], q_cos[:, :], q_sin[:, :], ALU.add).then_inc(s["qr"], 1)
                if p == AT["out"]:
                    since(pool, "oz", a + 1)
                    pool.tensor_tensor(res[:, :, :], oz[:, :, :], x[:, :, :], ALU.add).then_inc(s["res"], 1)
                if p == AT["norm1"]:
                    power(0, a, "ve1", "rs1")
                if p == AT["norm2"]:
                    power(1, a, "ve2", "rs2")

            def cross(g, p):
                if p == AT["v1"]:
                    since(pool, "x1", g + 1)
                    pool.wait_ge(s["ld_xwide"], 16 * 3)
                    since(pool, "y2", g)
                    pool.tensor_tensor(x1_bo[:, :, :], x1[:, :, :], wide[:, 5:6, :].broadcast_to([P, B, P]), ALU.add).then_inc(s["x1_bo"], 1)
                if p == AT["v1"] + 1:
                    since(pool, "vh", g + 1)
                    pool.tensor_tensor(v_hl[:, :, :, 1, 0:HD], v1[:, :, :, :], v_hl[:, :, :, 0, 0:HD], ALU.subtract).then_inc(s["vl"], 1)
                for b in range(B):
                    if p == SCORES_T[b] + 1:
                        n = B * g + b
                        since(pool, "prob_h", n + 1)
                        since(pool, "av_p", n - 1)
                        c = slice(0, POOL_COLS)
                        pool.tensor_tensor(prob_l[:, b % 2, c], prob[:, c], prob_h[:, b % 2, c], ALU.subtract).then_inc(s["prob_l"], 1)
                if p == AT["wo"]:
                    power(2, g, "ve3", "rs3")

            def low_weights(p):
                for n, at in enumerate(LOW_W):
                    if p == at:
                        c = slice(n % 4 * E * HID // 4, (n % 4 + 1) * E * HID // 4)
                        pool.wait_ge(s["i_ws"], n + 1)
                        pool.tensor_tensor(w_low[n // 4][:, c], stages[n // 4][:, c], w_high[n // 4][:, c], ALU.subtract).then_inc(s["i_wl"], 1)

            def low(f, e):
                n = E * f + e
                since(pool, "hi", n + 1)
                pool.tensor_tensor(gl[:, e % RING, :, :], g32[:, e % 2, :, :], gh[:, e % RING, :, :], ALU.subtract).then_inc(s["lo"], 1)

            def body(f, g, a):
                for e in range(E):
                    if f is not None:
                        low(f, e)
                        if e == LAG and not first_group(f):
                            power(3, f - 1, "ve4", "rs4")
                    for p in (2 * e, 2 * e + 1):
                        if a is not None:
                            linear(a, p)
                        if g is not None:
                            cross(g, p)
                        if f is None:
                            low_weights(p if g is None else p + 2 * E)

            body(None, None, 0)
            body(None, 0, 1)
            body(0, 1, 2)
            with pool.Fori(1, GROUPS - 2) as f:
                body(f, f + 1, f + 2)
            body(GROUPS - 2, GROUPS - 1, None)
            body(GROUPS - 1, None, None)
            power(3, GROUPS - 1, "ve4", "rs4")

        @block.scalar
        def _(act):
            act.dma_start(cst[:, :], consts).then_inc(s["ld_c"], 16)
            for i, n in enumerate(("L0_attn_Wq", "L0_attn_Wk", "L0_attn_Wv")):
                act.dma_start(w_in[:, i, :], A[n]).then_inc(s["ld_in"], 16)
            act.dma_start(b1_in[:, :], A["L0_ffn_b1"].rearrange("e (h n) -> (e h) n", h=HALF)).then_inc(s["ld_in"], 16)
            for to, n in ((bq, "L0_attn_bq"), (xbq, "L0_xattn_bq"), (xbk, "L0_xattn_bk")):
                act.dma_start(to[:, :], A[n].rearrange("(n a) -> n a", a=1)).then_inc(s["ld_b"], 16)
            act.wait_ge(s["i_wt"], 1)
            act.copy(wq_t[:, :], bA[:, 0:P]).then_inc(s["i_wtc"], 1)
            act.copy(wkv_t[:, :, :], bA[:, P:3 * P].rearrange("p (i n) -> p i n", i=2)).then_inc(s["i_wtc"], 1)
            act.copy(b1[:, :, :], bA[:, 3 * P:3 * P + E * HALF].rearrange("p (e h) -> p e h", h=HALF)).then_inc(s["i_wtc"], 1)

            def high_weights(p):
                for n, at in enumerate(HIGH_W):
                    if p == at:
                        c = slice(n % 4 * E * HID // 4, (n % 4 + 1) * E * HID // 4)
                        act.wait_ge(s[("ld_w1", "ld_w2")[n // 4]], 16)
                        act.activation(w_high[n // 4][:, c], stages[n // 4][:, c], ACT.Copy, scale=WS).then_inc(s["i_wh"], 1)
                        act.wait_ge(s["i_wh"], n + 1)
                        act.activation(stages[n // 4][:, c], stages[n // 4][:, c], ACT.Copy, scale=WS).then_inc(s["i_ws"], 1)
                if p == HIGH_W[3] + 1:
                    act.wait_ge(s["i_rw"], 16)
                    act.activation(rwh[:, :], rw[:, :], ACT.Copy, scale=WS).then_inc(s["i_rwl"], 1)

            def linear(a, p):
                if p == AT["x_t"]:
                    since(act, "x_tp", a + 1)
                    act.copy(x_t[:, :], bE).then_inc(s["x_tc"], 1)
                if p == AT["q"]:
                    since(act, "q_p", a + 1)
                    act.wait_ge(s["ld_b"], 16 * 3)
                    since(act, "q", a)
                    act.activation(qg[:, :], bE, ACT.Gelu, bias=bq[:, :]).then_inc(s["qg"], 1)
                if p == AT["kv23"]:
                    since(act, "kb", 2 * (a + 1))
                    since(act, "k_cos", a)
                    since(act, "k_sin", 2 * a)
                    since(act, "k_mean_p", a)
                    act.activation(kg[:, :, :], kb[:, :, :], ACT.Gelu).then_inc(s["kg"], 1)

            def cross(g, p):
                if p == AT["cx_t"]:
                    since(act, "cx_tp", g + 1)
                    act.copy(cx_t[:, :], bB[:, 0:B * CTX]).then_inc(s["cx_tc"], 1)
                if p == AT["v1"]:
                    since(act, "x1_tp", g + 1)
                    act.copy(x1_t[:, :], bD).then_inc(s["x1_tc"], 1)
                if p == AT["k"]:
                    since(act, "k_p", g + 1)
                    act.activation(kx[:, 0, :], bB[:, 0:B * CTX], ACT.Identity, bias=xbk[:, :]).then_inc(s["kxh"], 1)
                    since(act, "q_xp", g + 1)
                    act.activation(qx[:, 0, :], bC, ACT.Identity, bias=xbq[:, :]).then_inc(s["qxh"], 1)
                if p == AT["k_rep"]:
                    since(act, "k_rep_p", g + 1)
                    act.copy(k_rep[:, 0:2, :], ps[:, 0:2, 0:B * CTX]).then_inc(s["k_rep"], 1)
                if p == AT["q_rep"]:
                    since(act, "q_rep_p", g + 1)
                    act.copy(q_rep[:, 0:2, :], ps[:, 0:2, :]).then_inc(s["q_rep"], 1)
                if p == MAX_T:
                    since(act, "mxt_p", g + 1)
                    act.copy(mx_t[:, :], bA[:, 0:B * P // 2].bitcast(BF16)).then_inc(s["mxt_c"], 1)
                for b in range(B):
                    n = B * g + b
                    if p == SCORES_T[b]:
                        since(act, "t_p", n + 1)
                        since(act, "prob_l", 2 * n)
                        act.activation(prob[:, :].rearrange("p (r n) -> p r n", r=4), ps[0:CTX, 0:4, :],
                                       ACT.Exp, scale=float(HD) ** -0.5).then_inc(s["prob"], 1)
                if p == AT["ao_t"]:
                    since(act, "ao_tp", g + 1)
                    act.copy(ao_t[:, :], bA).then_inc(s["ao_tc"], 1)
                if p == AT["wo"] + 2:
                    since(act, "x2_tp", g + 1)
                    since(act, "h_p", HALF * E * g)
                    since(act, "lg_p", g)
                    act.copy(x2h[:, :], bA).then_inc(s["x2h"], 1)

            def router(f, p):
                if p == AT["weights"]:
                    since(act, "lgm", f + 1)
                    act.activation(th[:, :, :], lgm[:, :, :], ACT.Tanh, scale=0.5).then_inc(s["th"], 1)
                if p == AT["c_t"]:
                    since(act, "cw_tp", f + 1)
                    act.copy(cw_t[:, :], ps[0:E, 4, :]).then_inc(s["cw_tc"], 1)

            def gelu(f, e):
                n = E * f + e
                for h in range(HALF):
                    since(act, "h_p", HALF * n + h + 1)
                    if h == 0:
                        since(act, "lo", n - 1)
                    act.activation(g32[:, e % 2, h, :], bH[:, h, :], ACT.Gelu, bias=b1[:, e, h:h + 1], scale=1.0 / WS).then_inc(s["gelu"], 1)

            def body(f, g, a):
                for e in range(E):
                    if f is not None:
                        gelu(f, e)
                    for p in (2 * e, 2 * e + 1):
                        if f is not None:
                            router(f, p)
                        if a is not None:
                            linear(a, p)
                        if g is not None:
                            cross(g, p)
                        if f is None:
                            high_weights(p if g is None else p + 2 * E)

            body(None, None, 0)
            body(None, 0, 1)
            body(0, 1, 2)
            with act.Fori(1, GROUPS - 2) as f:
                body(f, f + 1, f + 2)
            body(GROUPS - 2, GROUPS - 1, None)
            body(GROUPS - 1, None, None)

        @block.tensor
        def _(pe):
            pe.wait_ge(s["ld_c"], 16)
            pe.wait_ge(s["ld_in"], 16 * 4)
            for i in range(3):
                pe.transpose(bA[:, i * P:(i + 1) * P], w_in[:, i, :], ident)
            pe.transpose(bA[:, 3 * P:3 * P + E * HALF], b1_in[:, :], ident[0:E * HALF, 0:E * HALF]).then_inc(s["i_wt"], 1)

            def linear(a, p):
                if p == AT["x_t"]:
                    pe.wait_ge(s["ld_x"], 16 * (a + 1))
                    since(pe, "oz", a)
                    since(pe, "av", B * (a - 1))
                    for b in range(B):
                        m = pe.transpose(bE[:, b * P:(b + 1) * P], x[:, b, :], ident)
                    m.then_inc(s["x_tp"], 1)
                if p == AT["q"]:
                    pe.wait_ge(s["i_wtc"], 3)
                    since(pe, "x_tc", a + 1)
                    pe.matmul(bE, wq_t[:, :], x_t[:, :], start=True, stop=True).then_inc(s["q_p"], 1)
                for j in range(2):
                    if p == AT[("kv01", "kv23")[j]]:
                        if j == 0:
                            since(pe, "qg", a + 1)
                        else:
                            since(pe, "v", 2 * a + 1)
                        for b in range(2):
                            m = pe.matmul(bE[:, b * 2 * P:(b + 1) * 2 * P], x_t[:, (2 * j + b) * P:(2 * j + b + 1) * P],
                                          wkv_t[:, :, :], start=True, stop=True)
                        m.then_inc(s[("kv01_p", "kv23_p")[j]], 1)
                if p == AT["rot"]:
                    since(pe, "q", a + 1)
                    since(pe, "v", 2 * (a + 1))
                    pe.matmul(bE, c_("rot"), q[:, :], start=True, stop=True).then_inc(s["rot_p"], 1)
                if p == AT["k_mean"]:
                    since(pe, "kg", a + 1)
                    since(pe, "q_sin", a + 1)
                    pe.wait_ge(s["i_ones"], 2)
                    for b in range(B):
                        m = pe.matmul(bE[:, b:b + 1], kg[:, b, :], mean_col[:, :], start=True, stop=True)
                    m.then_inc(s["k_mean_p"], 1)
                if p == AT["kv"]:
                    since(pe, "kr", a + 1)
                    since(pe, "k_mean", a + 1)
                    for b in range(B):
                        m = pe.matmul(bE[:, b * P:(b + 1) * P], kr[:, b, :], v[:, b, :], start=True, stop=True)
                    m.then_inc(s["kv_p"], 1)
                if p == AT["den"]:
                    since(pe, "kv", a + 1)
                    for b in range(B):
                        m = pe.matmul(bE[:, b * HEADS:(b + 1) * HEADS], q[:, b * P:(b + 1) * P], k_mean[:, b, :], start=True, stop=True)
                    m.then_inc(s["d_p"], 1)
                if p == AT["out"]:
                    since(pe, "den", a + 1)
                    since(pe, "qr", a + 1)
                    for b in range(B):
                        m = pe.matmul(bE[:, b * P:(b + 1) * P], qr[:, b * P:(b + 1) * P], kv[:, b, :], start=True, stop=True)
                    m.then_inc(s["out_p"], 1)

            def cross(g, p):
                if p == AT["cx_t"]:
                    pe.wait_ge(s["ld_cx"], 16 * (g + 1))
                    pe.wait_ge(s["i_wtc"], 3)
                    since(pe, "y2", g)
                    for b in range(B):
                        m = pe.transpose(bB[:, b * CTX:(b + 1) * CTX], cx[:, b, :], ident[0:CTX, 0:CTX])
                    m.then_inc(s["cx_tp"], 1)
                if p == AT["v1"]:
                    since(pe, "cx_tc", g + 1)
                    since(pe, "prob", B * g)
                    pe.wait_ge(s["ld_xw"], 16 * 4)
                    for b in range(B):
                        m = pe.matmul(bC[0:CTX, b * P:(b + 1) * P], cx_t[:, b * CTX:(b + 1) * CTX], xw[:, 2, :], start=True, stop=True)
                    m.then_inc(s["v1_p"], 1)
                    since(pe, "x1", g + 1)
                    for b in range(B):
                        m = pe.transpose(bD[:, b * P:(b + 1) * P], x1[:, b, :], ident)
                    m.then_inc(s["x1_tp"], 1)
                if p == AT["k"]:
                    pe.matmul(bB[:, 0:B * CTX], xw[:, 1, :], cx_t[:, :], start=True, stop=True).then_inc(s["k_p"], 1)
                    since(pe, "v1", g + 1)
                    since(pe, "x1_tc", g + 1)
                    pe.matmul(bC, xw[:, 0, :], x1_t[:, :], start=True, stop=True).then_inc(s["q_xp"], 1)
                if p == AT["k_rep"]:
                    since(pe, "lg", g)
                    since(pe, "kxl", g + 1)
                    since(pe, "qxl", g + 1)
                    pe.wait_ge(s["i_rep"], 8)
                    for i in range(BLK):
                        pe.matmul(ps[:, i, 0:B * CTX], rep4[:, 1, 0, i, :, :, :], kx[:, 0, :], start=True, stop=False)
                        m = pe.matmul(ps[:, i, 0:B * CTX], rep4[:, 1, 1, i, :, :, :], kx[:, 1, :], start=False, stop=True)
                    m.then_inc(s["k_rep_p"], 1)
                if p == AT["q_rep"]:
                    since(pe, "k_rep", 2 * (g + 1))
                    for i in range(BLK):
                        pe.matmul(ps[:, i, :], rep4[:, 0, 0, i, :, :, :], qx[:, 0, :], start=True, stop=False)
                        m = pe.matmul(ps[:, i, :], rep4[:, 0, 1, i, :, :, :], qx[:, 1, :], start=False, stop=True)
                    m.then_inc(s["q_rep_p"], 1)
                if p == MAX_T:
                    since(pe, "mxl", g + 1)
                    pe.wait_ge(s["i_idb"], 2)
                    for b in range(B):
                        m = pe.transpose(bA[:, b * P // 2:(b + 1) * P // 2].bitcast(BF16), mx_hl[:, b, :, :, :], identb[:, :])
                    m.then_inc(s["mxt_p"], 1)
                for b in range(B):
                    if p == VALUES[b]:
                        values(g, b)
                    if p == SCORES[b]:
                        scores(g, b)
                    if p == SCORES_T[b]:
                        scores_t(g, b)
                if p == AT["ao_t"]:
                    since(pe, "ao", B * (g + 1))
                    for b in range(B):
                        m = pe.transpose(bA[:, b * P:(b + 1) * P], ao[:, b, :], ident)
                    m.then_inc(s["ao_tp"], 1)
                if p == AT["wo"]:
                    since(pe, "ao_tc", g + 1)
                    for b in range(B):
                        m = pe.matmul(bB[:, b * P:(b + 1) * P], ao_t[:, b * P:(b + 1) * P], xw[:, 3, :], start=True, stop=True)
                    m.then_inc(s["wo_p"], 1)
                if p == AT["wo"] + 2:
                    since(pe, "x2n", g + 1)
                    for b in range(B):
                        m = pe.transpose(bA[:, b * P:(b + 1) * P], x2n[:, b, :], ident)
                    m.then_inc(s["x2_tp"], 1)

            def scores(g, b):
                if b == 0:
                    since(pe, "q_rep", 2 * (g + 1))
                else:
                    since(pe, "mx", B * g + b)
                for i in range(BLK):
                    for r in range(4):
                        m = pe.matmul(ps[:, r, i * CTX:(i + 1) * CTX], q_rep[32 * r:32 * r + 32, i, b * P:(b + 1) * P],
                                      k_rep[32 * r:32 * r + 32, i, b * CTX:(b + 1) * CTX], start=True, stop=True)
                m.then_inc(s["s_p"], 1)

            def scores_t(g, b):
                n = B * g + b
                if b == 0:
                    since(pe, "mxt_c", g + 1)
                since(pe, "prob", n)
                for i in range(BLK):
                    for r in range(4):
                        pe.matmul(ps[0:CTX, r, i * P:(i + 1) * P], k_rep[32 * r:32 * r + 32, i, b * CTX:(b + 1) * CTX],
                                  q_rep[32 * r:32 * r + 32, i, b * P:(b + 1) * P], start=True, stop=False)
                    for r in range(4):
                        m = pe.matmul(ps[0:CTX, r, i * P:(i + 1) * P], pick[32 * r:32 * r + 32, i, :],
                                      mx_t[32 * r:32 * r + 32, b * P:(b + 1) * P], start=False, stop=True)
                m.then_inc(s["t_p"], 1)

            def values(g, b):
                n = B * g + b
                W = HD + 1
                since(pe, "prob_l", 2 * (n + 1))
                since(pe, "vl", g + 1)
                pe.wait_ge(s["i_v1"], 2)
                if b == 0:
                    since(pe, "oz", min_groups(g + 2))
                    since(pe, "acc_b2", g)
                since(pe, "av", n)
                for r in range(4):
                    for i in range(BLK):
                        at, to = (4 * r + i) * P, 2 * W * (4 * i + r)
                        pe.matmul(bE[:, to:to + 2 * W], prob_h[:, b % 2, at:at + P], v_hl[:, b, 4 * i + r, :, :], start=True, stop=False)
                        m = pe.matmul(bE[:, to:to + W], prob_l[:, b % 2, at:at + P], v_hl[:, b, 4 * i + r, 0, :], start=False, stop=True)
                m.then_inc(s["av_p"], 1)

            def router(f, p):
                if p == AT["logits"]:
                    since(pe, "x2l", f + 1)
                    pe.wait_ge(s["i_rwl"], 2)
                    for b in range(B):
                        o = bA[:, b * E:(b + 1) * E]
                        xh, xl = x2h[:, b * P:(b + 1) * P], x2l[:, b * P:(b + 1) * P]
                        pe.matmul(o, xh, rwh[:, :], start=True, stop=False)
                        pe.matmul(o, xh, rwl[:, :], start=False, stop=False)
                        pe.matmul(o, xl, rwh[:, :], start=False, stop=False)
                        m = pe.matmul(o, xl, rwl[:, :], start=False, stop=True)
                    m.then_inc(s["lg_p"], 1)
                if p == AT["c_t"]:
                    since(pe, "cw", f + 1)
                    since(pe, "oz", min_groups(f + 3))
                    for b in range(B):
                        m = pe.transpose(ps[0:E, 4, b * P:(b + 1) * P], cw[:, b, :], ident)
                    m.then_inc(s["cw_tp"], 1)
                if p == AT["b2"]:
                    since(pe, "cw_tc", f + 1)
                    pe.wait_ge(s["i_b2"], 16)
                    for b in range(B):
                        m = pe.matmul(bE[:, b * P:(b + 1) * P], cw_t[:, b * P:(b + 1) * P], b2[:, :], start=True, stop=True)
                    m.then_inc(s["b2_p"], 1)

            def first(f, e):
                n = E * f + e
                if e == 0:
                    since(pe, "x2l", f + 1)
                for h in range(HALF):
                    since(pe, "gelu", HALF * (n - 1) + h + 1)
                    wh, wl = w1h[:, e, h * P:(h + 1) * P], w1l[:, e, h * P:(h + 1) * P]
                    pe.matmul(bH[:, h, :], wh, x2h[:, :], start=True, stop=False)
                    pe.matmul(bH[:, h, :], wh, x2l[:, :], start=False, stop=False)
                    pe.matmul(bH[:, h, :], wl, x2h[:, :], start=False, stop=True).then_inc(s["h_p"], 1)

            def second(f, e):
                n = E * f + e
                since(pe, "lo", n + 1)
                since(pe, "comb", n)
                for b in range(B):
                    for h in range(HALF):
                        o = bY[:, b * P:(b + 1) * P]
                        ghb, glb = gh[:, e % RING, h, b * P:(b + 1) * P], gl[:, e % RING, h, b * P:(b + 1) * P]
                        pe.matmul(o, ghb, w2h[:, e, h, :], start=(h == 0), stop=False)
                        pe.matmul(o, ghb, w2l[:, e, h, :], start=False, stop=False)
                        m = pe.matmul(o, glb, w2h[:, e, h, :], start=False, stop=(h == HALF - 1))
                m.then_inc(s["y_p"], 1)

            def body(f, g, a):
                for e in range(E):
                    if f is not None and e > 0:
                        first(f, e)
                    for p in (2 * e, 2 * e + 1):
                        if a is not None:
                            linear(a, p)
                        if g is not None:
                            cross(g, p)
                        if f is not None and p % 2 == 0:
                            if e >= LAG:
                                second(f, e - LAG)
                            elif not first_group(f):
                                second(f - 1, E - LAG + e)
                        if f is not None:
                            if p == 0:
                                first(f, 0)
                            router(f, p)

            body(None, None, 0)
            body(None, 0, 1)
            pe.wait_ge(s["i_wl"], 8)
            body(0, 1, 2)
            with pe.Fori(1, GROUPS - 2) as f:
                body(f, f + 1, f + 2)
            body(GROUPS - 2, GROUPS - 1, None)
            body(GROUPS - 1, None, None)
            for e in range(E - LAG, E):
                second(GROUPS - 1, e)

        @block.vector
        def _(dve):
            def low_router():
                dve.wait_ge(s["i_rwl"], 1)
                dve.scalar_tensor_tensor(out=rwl[:, :], in0=rw[:, :], scalar=WS, in1=rwh[:, :], op0=ALU.mult, op1=ALU.subtract).then_inc(s["i_rwl"], 1)

            def static_wait():
                dve.wait_ge(s["ld_c"], 16)

            def wide_b(ap, n=B):
                return ap.rearrange("p (a n) -> p a n", a=1).broadcast_to([P, n, ap.shape[1]])

            def by_seq(ap):
                return ap[:, :].rearrange("p (b n) -> p b n", b=B)

            def moments(k, src, g, used, st, ag, vn, eps):
                since(dve, used, g)
                for b in range(B):
                    m = dve.bn_stats(stats[:, k, b, :], src[:, b, :])
                m.then_inc(s[st], 1)
                static_wait()
                since(dve, st, g + 1)
                for b in range(B):
                    m = dve.bn_aggr(mv[:, k, b, :], stats[:, k, b, :])
                m.then_inc(s[ag], 1)
                since(dve, ag, g + 1)
                dve.tensor_scalar(ve[:, k, :], mv[:, k, :, 1], eps, None, ALU.add).then_inc(s[vn], 1)

            def linear(a, p):
                if p == AT["q"]:
                    since(dve, "qg", a + 1)
                    since(dve, "rot_p", a)
                    since(dve, "d_p", a)
                    dve.tensor_scalar(q[:, :], qg[:, :], 0.21, None, ALU.add).then_inc(s["q"], 1)
                    since(dve, "q", a + 1)
                    since(dve, "qr", a)
                    dve.tensor_tensor(by_seq(q_cos), by_seq(q), wide_b(c_("cos_t")), ALU.mult).then_inc(s["q_cos"], 1)
                for j in range(2):
                    if p == AT[("kv01", "kv23")[j]]:
                        since(dve, ("kv01_p", "kv23_p")[j], a + 1)
                        since(dve, "kg", a)
                        if j == 0:
                            dve.wait_ge(s["ld_wide"], 16 * 4)
                            since(dve, "kv_p", a)
                        both = bE.rearrange("p (b i n) -> p b i n", b=2, i=2)
                        dve.tensor_tensor(kb[:, 2 * j:2 * j + 2, :], both[:, :, 0, :], wide_b(wide[:, 0, :], 2), ALU.add).then_inc(s["kb"], 1)
                        dve.tensor_tensor(v[:, 2 * j:2 * j + 2, :], both[:, :, 1, :], wide_b(wide[:, 1, :], 2), ALU.add).then_inc(s["v"], 1)
                if p == AT["kv23"] + 1:
                    since(dve, "kg", a + 1)
                    since(dve, "kr", a)
                    dve.scalar_tensor_tensor(out=k_cos[:, :, :], in0=kg[:, :, :], scalar=0.21, in1=wide_b(c_("cos")), op0=ALU.add, op1=ALU.mult).then_inc(s["k_cos"], 1)
                    for to, name in ((0, "sin_neg"), (1, "sin")):
                        dve.scalar_tensor_tensor(out=k_sin[:, :, to::2], in0=kg[:, :, 1 - to::2], scalar=0.21, in1=wide_b(c_(name)),
                                                 op0=ALU.add, op1=ALU.mult).then_inc(s["k_sin"], 1)
                if p == AT["rot"]:
                    since(dve, "rot_p", a + 1)
                    since(dve, "qr", a)
                    dve.tensor_tensor(by_seq(q_sin), by_seq(bE), wide_b(c_("sin_t")), ALU.mult).then_inc(s["q_sin"], 1)
                if p == AT["k_mean"]:
                    since(dve, "k_mean_p", a + 1)
                    since(dve, "d_p", a)
                    dve.scalar_tensor_tensor(out=k_mean[:, :, :], in0=bE[:, 0:B].rearrange("p (b a) -> p b a", a=1).broadcast_to([P, B, HEADS]),
                                             scalar=0.21, in1=wide_b(c_("head_of")), op0=ALU.add, op1=ALU.mult).then_inc(s["k_mean"], 1)
                if p == AT["kv"]:
                    since(dve, "kv_p", a + 1)
                    since(dve, "out_p", a)
                    dve.tensor_tensor(kv[:, :, :], by_seq(bE), wide_b(c_("same_head")), ALU.mult).then_inc(s["kv"], 1)
                if p == AT["den"]:
                    since(dve, "d_p", a + 1)
                    dve.tensor_scalar(den[:, :], bE[:, 0:B * HEADS], 1e-6, None, ALU.add).then_inc(s["den"], 1)
                    since(dve, "den", a + 1)
                    since(dve, "oz", a)
                    dve.reciprocal(z[:, :], den[:, :]).then_inc(s["z"], 1)
                if p == AT["out"]:
                    since(dve, "out_p", a + 1)
                    since(dve, "z", a + 1)
                    since(dve, "res", a)
                    dve.tensor_tensor(oz[:, :, :].rearrange("p b (h d) -> p (b h) d", d=HD), bE.rearrange("p (n d) -> p n d", d=HD),
                                      z[:, :].rearrange("p (n a) -> p n a", a=1).broadcast_to([P, B * HEADS, HD]), ALU.mult).then_inc(s["oz"], 1)
                if p == AT["norm1"]:
                    since(dve, "res", a + 1)
                    moments(0, res, a, "y1", "st1", "ag1", "ve1", 1e-12)
                    for b in range(B):
                        m = dve.scalar_tensor_tensor(out=resg[:, b, :], in0=res[:, b, :], scalar=mv[:, 0, b, 0:1], in1=wide[:, 2, :],
                                                     op0=ALU.subtract, op1=ALU.mult)
                    m.then_inc(s["resg"], 1)
                if p == AT["norm2"]:
                    since(dve, "rs1", a + 1)
                    since(dve, "resg", a + 1)
                    since(dve, "x_beta", a + 1)
                    since(dve, "x1", a)
                    for b in range(B):
                        m = dve.scalar_tensor_tensor(out=y1[:, b, :], in0=resg[:, b, :], scalar=rstd[:, 0, b:b + 1], in1=x_beta[:, b, :],
                                                     op0=ALU.mult, op1=ALU.add)
                    m.then_inc(s["y1"], 1)
                    since(dve, "y1", a + 1)
                    moments(1, y1, a, "x1", "st2", "ag2", "ve2", 1e-5)
                if p == AT["x1"]:
                    since(dve, "rs2", a + 1)
                    since(dve, "x1_bo", a)
                    since(dve, "x1_tp", a)
                    for b in range(B):
                        m = dve.tensor_scalar(x1[:, b, :], y1[:, b, :], mv[:, 1, b, 0:1], rstd[:, 1, b:b + 1], ALU.subtract, ALU.mult)
                    m.then_inc(s["x1"], 1)

            def cross(g, p):
                if p == AT["v1"]:
                    since(dve, "v1_p", g + 1)
                    dve.wait_ge(s["ld_xwide"], 16 * 3)
                    since(dve, "vl", g)
                    dve.tensor_tensor(v1[:, :, :, :].rearrange("p b h d -> p b (h d)"), bC[0:CTX, :].rearrange("p (b n) -> p b n", b=B),
                                      wide[0:CTX, 4:5, :].broadcast_to([CTX, B, P]), ALU.add).then_inc(s["v1"], 1)
                    since(dve, "v1", g + 1)
                    since(dve, "av_p", B * g)
                    dve.tensor_copy(v_hl[:, :, :, 0, 0:HD], v1[:, :, :, :]).then_inc(s["vh"], 1)
                if p == AT["k"]:
                    since(dve, "kxh", g + 1)
                    since(dve, "k_rep_p", g)
                    dve.scalar_tensor_tensor(out=kx[:, 1, :], in0=bB[:, 0:B * CTX], scalar=xbk[:, :], in1=kx[:, 0, :],
                                             op0=ALU.add, op1=ALU.subtract).then_inc(s["kxl"], 1)
                    since(dve, "qxh", g + 1)
                    since(dve, "q_rep_p", g)
                    dve.scalar_tensor_tensor(out=qx[:, 1, :], in0=bC, scalar=xbq[:, :], in1=qx[:, 0, :],
                                             op0=ALU.add, op1=ALU.subtract).then_inc(s["qxl"], 1)
                if p == AT["k_rep"]:
                    since(dve, "k_rep_p", g + 1)
                    since(dve, "t_p", B * g)
                    dve.tensor_copy(k_rep[:, 2:4, :], ps[:, 2:4, 0:B * CTX]).then_inc(s["k_rep"], 1)
                if p == AT["q_rep"]:
                    since(dve, "q_rep_p", g + 1)
                    dve.tensor_copy(q_rep[:, 2:4, :], ps[:, 2:4, :]).then_inc(s["q_rep"], 1)
                if p == MAX_T - 1:
                    since(dve, "mx", B * (g + 1))
                    since(dve, "mxt_p", g)
                    mxb = mx[:, :, :].rearrange("p b (a h) -> p b a h", a=1).broadcast_to([P, B, 4, HEADS])
                    dve.tensor_copy(mx_hl[:, :, :, 0, :], mxb).then_inc(s["mxh"], 1)
                    since(dve, "mxh", g + 1)
                    dve.tensor_tensor(mx_hl[:, :, :, 1, :], mxb, mx_hl[:, :, :, 0, :], ALU.subtract).then_inc(s["mxl"], 1)
                for b in range(B):
                    n = B * g + b
                    if p == SCORES[b]:
                        since(dve, "s_p", n + 1)
                        since(dve, "mxl", g)
                        dve.tensor_reduce(mx[:, b, :].rearrange("p (r i) -> p r i", r=4),
                                          ps[:, 0:4, 0:BLK * CTX].rearrange("p r (i k) -> p r i k", i=BLK), AX.X, ALU.max).then_inc(s["mx"], 1)
                    if p == SCORES_T[b] + 1:
                        since(dve, "prob", n + 1)
                        since(dve, "av_p", n - 1)
                        dve.tensor_copy(prob_h[:, b % 2, :], prob[:, :]).then_inc(s["prob_h"], 1)
                        since(dve, "prob_h", n + 1)
                        c = slice(POOL_COLS, HEADS * P)
                        dve.tensor_tensor(prob_l[:, b % 2, c], prob[:, c], prob_h[:, b % 2, c], ALU.subtract).then_inc(s["prob_l"], 1)
                    if p == VALUES[b]:
                        normalize(g, b)
                if p == AT["wo"]:
                    since(dve, "wo_p", g + 1)
                    since(dve, "x1_bo", g + 1)
                    since(dve, "x2n", g)
                    dve.tensor_tensor(y2[:, :, :], by_seq(bB), x1_bo[:, :, :], ALU.add).then_inc(s["y2"], 1)
                    since(dve, "y2", g + 1)
                    moments(2, y2, g, "x2n", "st3", "ag3", "ve3", 1e-5)
                if p == AT["wo"] + 1:
                    since(dve, "rs3", g + 1)
                    since(dve, "x2_tp", g)
                    if not (isinstance(g, int) and g == 0):
                        since(dve, "comb", E * (g - 1) + 1)
                    for b in range(B):
                        m = dve.tensor_scalar(x2n[:, b, :], y2[:, b, :], mv[:, 2, b, 0:1], rstd[:, 2, b:b + 1], ALU.subtract, ALU.mult)
                    m.then_inc(s["x2n"], 1)
                if p == AT["wo"] + 2:
                    since(dve, "x2h", g + 1)
                    dve.tensor_tensor(x2l[:, :], bA, x2h[:, :], ALU.subtract).then_inc(s["x2l"], 1)

            def normalize(g, b):
                n = B * g + b
                W = HD + 1
                since(dve, "av_p", n + 1)
                since(dve, "ao", n)
                dve.tensor_reduce(av[:, :, :], bE[:, 0:2 * W * HEADS].rearrange("p (h t d) -> p h d t", t=2, d=W),
                                  AX.X, ALU.add).then_inc(s["av"], 1)
                since(dve, "av", n + 1)
                dve.reciprocal(rs[:, :], av[:, :, HD]).then_inc(s["rs_"], 1)
                since(dve, "rs_", n + 1)
                since(dve, "ao_tp", g)
                dve.tensor_tensor(ao[:, b, :].rearrange("p (h d) -> p h d", d=HD), av[:, :, 0:HD],
                                  rs[:, :].rearrange("p (h a) -> p h a", a=1).broadcast_to([P, HEADS, HD]), ALU.mult).then_inc(s["ao"], 1)

            def router(f, p):
                if p == AT["logits"]:
                    since(dve, "lg_p", f + 1)
                    dve.wait_ge(s["i_lg"], 1)
                    since(dve, "chosen", f)
                    since(dve, "lgm", f)
                    dve.scalar_tensor_tensor(out=lg[:, :, 0:E], in0=bA[:, 0:B * E].rearrange("p (b e) -> p b e", b=B), scalar=1.0 / WS,
                                             in1=wide_b(rb[:, :]), op0=ALU.mult, op1=ALU.add).then_inc(s["lg"], 1)
                    static_wait()
                    since(dve, "lg", f + 1)
                    since(dve, "cut", f)
                    for b in range(B):
                        m = dve.max(top[:, b, :], lg[:, b, :])
                    m.then_inc(s["top"], 1)
                    since(dve, "top", f + 1)
                    since(dve, "th", f)
                    dve.tensor_tensor(lgm[:, :, :], lg[:, :, 0:E], top[:, :, 0:1].broadcast_to([P, B, E]), ALU.subtract).then_inc(s["lgm"], 1)
                    since(dve, "lgm", f + 1)
                    dve.memset(top[:, :, TOPK:8], FAR).then_inc(s["topx"], 1)
                    static_wait()
                    since(dve, "topx", f + 1)
                    for b in range(B):
                        m = dve.match_replace(cut[:, b, :], top[:, b, :], lg[:, b, :], -FAR)
                    m.then_inc(s["cut"], 1)
                    since(dve, "cut", f + 1)
                    since(dve, "pm", f)
                    dve.tensor_tensor(chosen[:, :, :], cut[:, :, 0:E], lg[:, :, 0:E], ALU.not_equal).then_inc(s["chosen"], 1)
                if p == AT["weights"]:
                    since(dve, "th", f + 1)
                    since(dve, "chosen", f + 1)
                    dve.tensor_scalar(dnm[:, :, :], th[:, :, :], -1.0, 1.0, ALU.mult, ALU.add).then_inc(s["dnm"], 1)
                    dve.scalar_tensor_tensor(out=num[:, :, :], in0=th[:, :, :], scalar=1.0, in1=chosen[:, :, :], op0=ALU.add, op1=ALU.mult).then_inc(s["num"], 1)
                    since(dve, "dnm", f + 1)
                    dve.reciprocal(rdn[:, :, :], dnm[:, :, :]).then_inc(s["rdn"], 1)
                    since(dve, "rdn", f + 1)
                    since(dve, "num", f + 1)
                    dve.tensor_tensor(pm[:, :, :], num[:, :, :], rdn[:, :, :], ALU.mult).then_inc(s["pm"], 1)
                    since(dve, "pm", f + 1)
                    dve.tensor_reduce(ps_[:, :], pm[:, :, :], AX.X, ALU.add).then_inc(s["ps_"], 1)
                    since(dve, "ps_", f + 1)
                    dve.tensor_scalar(ps2[:, :], ps_[:, :], WS, None, ALU.mult).then_inc(s["ps2"], 1)
                    since(dve, "ps2", f + 1)
                    dve.reciprocal(rps[:, :], ps2[:, :]).then_inc(s["rps"], 1)
                if p == 2 * LAG:
                    since(dve, "rps", f + 1)
                    since(dve, "comb", E * f)
                    since(dve, "cw_tp", f)
                    dve.tensor_tensor(cw[:, :, :], pm[:, :, :], rps[:, :].rearrange("p (b a) -> p b a", a=1).broadcast_to([P, B, E]), ALU.mult).then_inc(s["cw"], 1)
                if p == AT["acc_b2"]:
                    since(dve, "b2_p", f + 1)
                    since(dve, "comb", E * f + (p + 1) // 2 - LAG)
                    dve.scalar_tensor_tensor(out=acc[:, :, :], in0=by_seq(bE), scalar=WS, in1=acc[:, :, :], op0=ALU.mult, op1=ALU.add).then_inc(s["acc_b2"], 1)

            def high(f, e):
                n = E * f + e
                since(dve, "gelu", HALF * (n + 1))
                back = n - RING + 1
                if not (isinstance(back, int) and back <= 0):
                    since(dve, "y_p", back)
                dve.tensor_copy(gh[:, e % RING, :, :], g32[:, e % 2, :, :]).then_inc(s["hi"], 1)

            def combine(f, e):
                n = E * f + e
                since(dve, "y_p", n + 1)
                if e == 0:
                    since(dve, "cw", f + 1)
                    since(dve, "x2n", f + 1)
                since(dve, "comb", n)
                since(dve, "acc_b2", f + 1 if 2 * (e + LAG) >= AT["acc_b2"] else f)
                for b in range(B):
                    m = dve.scalar_tensor_tensor(out=(acc_all if e == E - 1 else acc)[:, b, :], in0=bY[:, b * P:(b + 1) * P],
                                                 scalar=cw[:, b, e:e + 1], in1=(acc if e else x2n)[:, b, :], op0=ALU.mult, op1=ALU.add)
                m.then_inc(s["comb"], 1)

            def sum_moments(f):
                since(dve, "comb", E * (f + 1))
                moments(3, acc_all, f, "fin", "st4", "ag4", "ve4", 1e-5)

            def finish(f):
                since(dve, "rs4", f + 1)
                since(dve, "st_out", 16 * f)
                for b in range(B):
                    m = dve.tensor_scalar(fin[:, b, :], acc_all[:, b, :], mv[:, 3, b, 0:1], rstd[:, 3, b:b + 1], ALU.subtract, ALU.mult)
                m.then_inc(s["fin"], 1)

            def body(f, g, a):
                for e in range(E):
                    if f is not None:
                        high(f, e)
                    for p in (2 * e, 2 * e + 1):
                        if f is not None:
                            router(f, p)
                        if a is not None:
                            linear(a, p)
                        if g is not None:
                            cross(g, p)
                        if f is not None and p % 2 == 0:
                            if e >= LAG:
                                combine(f, e - LAG)
                            elif not first_group(f):
                                combine(f - 1, E - LAG + e)
                                if e == LAG - 1:
                                    sum_moments(f - 1)
                        if f is not None and p == 2 * LAG + 2 and not first_group(f):
                            finish(f - 1)

            body(None, None, 0)
            low_router()
            body(None, 0, 1)
            body(0, 1, 2)
            with dve.Fori(1, GROUPS - 2) as f:
                body(f, f + 1, f + 2)
            body(GROUPS - 2, GROUPS - 1, None)
            body(GROUPS - 1, None, None)
            for e in range(E - LAG, E):
                combine(GROUPS - 1, e)
            sum_moments(GROUPS - 1)
            finish(GROUPS - 1)


_INS = ['x', 'ctx_1024', 'L0_attn_Wq', 'L0_attn_bq', 'L0_attn_Wk', 'L0_attn_bk', 'L0_attn_Wv', 'L0_attn_bv', 'L0_attn_gamma',
        'L0_attn_beta', 'L0_xattn_Wq', 'L0_xattn_bq', 'L0_xattn_Wk', 'L0_xattn_bk', 'L0_xattn_Wv', 'L0_xattn_bv', 'L0_xattn_Wo',
        'L0_xattn_bo', 'L0_ffn_router_w', 'L0_ffn_router_b', 'L0_ffn_w1', 'L0_ffn_b1', 'L0_ffn_w2', 'L0_ffn_b2']


def kernel(**inputs):
    import numpy as _np
    import concourse.bacc as _bacc
    from concourse import mybir as _mybir
    from concourse.bass_utils import run_bass_kernel_spmd as _run

    nc = _bacc.Bacc("TRN2", target_bir_lowering=False, num_devices=1)
    arrays, aps = {}, {}
    for name in _INS:
        a = _np.ascontiguousarray(inputs[name])
        arrays[f"in_{name}"] = a
        aps[name] = nc.dram_tensor(f"in_{name}", a.shape, _mybir.dt.from_np(a.dtype), kind="ExternalInput").ap()
    table, where = constants()
    arrays["constants"] = table
    consts = nc.dram_tensor("constants", table.shape, F32, kind="ExternalInput").ap()
    out = nc.dram_tensor("out", (SEQS, P, P), F32, kind="ExternalOutput").ap()
    build(nc, aps, consts, where, out)
    r = _run(nc, [arrays], core_ids=[0])
    return r.results[0]["out"]
```

```python
from contextlib import ExitStack

import numpy as np
import concourse.bass as bass
from concourse import mybir

ALU = mybir.AluOpType
ACT = mybir.ActivationFunctionType
AX = mybir.AxisListType
F32 = mybir.dt.float32
F16 = mybir.dt.float16

P = 128
B = 4
SEQS = 32
GROUPS = SEQS // B
T = B * P
CTX = 77
HEADS = 16
HD = 8
BLK = 4
E = 16
HID = 256
HALF = HID // P
TOPK = 4
LAG = 3
RING = 4
PLACES = 4
WS = 256.0
MAX_SCALE = 64.0
SETS = 4
MAX_ROWS = (3, 7)
SPREAD = 16 * (2 * 3 * BLK + 2)
FAR = -3.0e38
THETA = 10000.0


def constants():
    half = np.arange(0, P, 2, dtype=np.float32)
    inv = (np.float32(1.0) / np.float32(THETA) ** (half / np.float32(P))).astype(np.float32)
    ang = (np.arange(P, dtype=np.float32)[:, None] * inv).astype(np.float32)
    cos, sin = np.cos(ang).astype(np.float32), np.sin(ang).astype(np.float32)
    cos2, sin2 = np.repeat(cos, 2, axis=1), np.repeat(sin, 2, axis=1)
    ident = np.eye(P, dtype=np.float32)
    sin_t = sin2.T.copy()
    sin_t[0::2] *= -1.0
    ch = np.arange(P)
    same_head = (ch[:, None] // HD == ch[None, :] // HD).astype(np.float32) / P
    head_of = (ch[:, None] // HD == np.arange(HEADS)[None, :]).astype(np.float32)
    max_rows = np.zeros((P, 1), np.float32)
    for row in MAX_ROWS:
        max_rows[row::32] = -MAX_SCALE
    cols = dict(ident=ident, cos=cos2, sin_neg=-sin, sin=sin, cos_t=cos2.T, sin_t=sin_t,
                same_head=same_head, head_of=head_of,
                max_rows=max_rows)
    at, where = 0, {}
    for k, v in cols.items():
        where[k] = (at, v.shape[1])
        at += v.shape[1]
    return np.ascontiguousarray(np.concatenate(list(cols.values()), axis=1), np.float32), where


PE_AT = dict(x_t=0, q=2, kv01=7, kv23=7, k_mean=16, kv=21, den=27, out=32, cx_t=44, v1=46, x1_t=48,
             k=50, q_x=50, scores=(10, 12, 13, 16), max_t=20, scores_t=(24, 30, 36, 40), values=(36,
             40, 44, 48), ao_t=49, wo=53, x2_t=63, logits=1, c_t=48, b2=59, first=1, next=0,
             second=0)
ACT_AT = dict(x_t=0, q=4, kv23=10, cx_t=44, x1_t=45, k=49, q_x=50, max_t=20, scores_t=(24, 29, 37,
              40), ao_t=48, x2_t=63, weights=2, c_t=50, gelu=0, high=2)
DVE_AT = dict(q=2, kv01=4, kv23=5, k_rot=11, k_mean=15, kv=23, den=27, out=31, norm1=35, norm2=39,
              x1=44, v1=48, v_high=53, k=50, q_x=52, scores=(10, 12, 14, 16), max=20, parts=(30, 34,
              39, 42), values=(35, 40, 44, 48), wo=54, x2=59, x2_t=63, logits=1, weights=6, cw=9,
              b2=58, high=2, combine=0, finish=14, q_sin=14, sums=10)
POOL_AT = dict(x_beta=4, k_rot=11, q_rot=11, res=31, norm1=32, norm2=38, x1=7, v_low=53, parts=(28,
               35, 38, 38), x2=53, low=0, finish=10)
PE_EARLY = dict(x_t=0, q=3, kv01=4, kv23=8, k_mean=11, kv=21, den=25, out=29, cx_t=44, v1=46,
                x1_t=47, k=49, q_x=53, scores=(12, 12, 13, 15), max_t=23, scores_t=(25, 29, 35, 39),
                values=(34, 37, 41, 48), ao_t=48, wo=48, x2_t=63)
ACT_EARLY = dict(x_t=0, q=3, kv23=6, cx_t=44, x1_t=51, k=51, q_x=58, max_t=23, scores_t=(27, 30, 32,
                 42), ao_t=48, x2_t=63)
DVE_EARLY = dict(q=5, kv01=5, kv23=6, k_rot=8, k_mean=10, kv=19, den=25, out=31, norm1=34, norm2=36,
                 x1=42, v1=44, v_high=53, k=49, q_x=53, scores=(9, 12, 13, 14), max=20, parts=(28,
                 33, 37, 39), values=(36, 39, 41, 48), wo=48, x2=50, x2_t=63, q_sin=10)
POOL_EARLY = dict(x_beta=0, k_rot=10, q_rot=18, res=25, norm1=32, norm2=35, x1=3, v_low=51,
                  parts=(26, 33, 37, 43), x2=50)
HIGH_BY_ACT = (1, 2, 3, 4, 8, 10, 11, 12, 13, 14)
HIGH_W = (14, 15, 16, 17, 84, 85, 86, 93)
LOW_W = (14, 18, 25, 19, 74, 86, 86, 95)
POOL_COLS = 1280


def build(nc, A, consts, where, out):
    ctx = ExitStack()
    with ctx:
        def sb(name, shape, dt=F32):
            return ctx.enter_context(nc.sbuf_tensor(name, shape, dt))

        def sem(name):
            return ctx.enter_context(nc.semaphore(name))

        cst = sb("cst", [P, consts.shape[1]])

        def c_(name):
            a, n = where[name]
            return cst[:, a:a + n]

        ident = c_("ident")
        ident16 = sb("ident16", [P, P], F16)
        mean_col = sb("mean_col", [P, 1])
        half_pow = sb("half_pow", [P, B])
        w_in = sb("w_in", [P, 3, P])
        wq_t = sb("wq_t", [P, P])
        wkv_t = sb("wkv_t", [P, 2, P])
        xw = sb("xw", [P, 4, P])
        wide = sb("wide", [P, 6, P])
        rb = sb("rb", [P, E])
        bq = sb("bq", [P, 1])
        xbq = sb("xbq", [P, 1])
        xbk = sb("xbk", [P, 1])
        rw = sb("rw", [P, E])
        rwh = sb("rwh", [P, E], F16)
        rwl = sb("rwl", [P, E], F16)
        b1_in = sb("b1_in", [E * HALF, P])
        b1 = sb("b1", [P, E, HALF])
        b2 = sb("b2", [E, P])
        w_stage = sb("w_stage", [P, E * HID])
        prob = w_stage[0:CTX, :].rearrange("p (t n) -> p t n", t=2)
        w1h = sb("w1h", [P, E, HID], F16)
        w1l = sb("w1l", [P, E, HID], F16)
        w2h = sb("w2h", [P, E, HALF, P], F16)
        w2l = sb("w2l", [P, E, HALF, P], F16)
        x = sb("x", [P, B, P])
        cx = sb("cx", [CTX, B, P])
        x_t = sb("x_t", [P, T])
        cx_t = sb("cx_t", [P, B * CTX])
        qg = sb("qg", [P, T])
        q = sb("q", [P, T])
        q_cos = sb("q_cos", [P, T])
        q_swap = sb("q_swap", [P, T])
        q_sin = sb("q_sin", [P, T])
        qr = sb("qr", [P, T])
        kb = sb("kb", [P, B, P])
        v = sb("v", [P, B, P])
        kg = sb("kg", [P, B, P])
        k_cos = sb("k_cos", [P, B, P])
        k_sin = sb("k_sin", [P, B, P])
        kr = sb("kr", [P, B, P])
        k_mean = sb("k_mean", [P, B, HEADS])
        kv = sb("kv", [P, B, P])
        den = sb("den", [P, B * HEADS])
        z = sb("z", [P, B * HEADS])
        oz = sb("oz", [P, B, P])
        res = sb("res", [P, B, P])
        x_beta = sb("x_beta", [P, B, P])
        resg = sb("resg", [P, B, P])
        y1 = sb("y1", [P, B, P])
        x1 = sb("x1", [P, B, P])
        x1_bo = sb("x1_bo", [P, B, P])
        x1_t = sb("x1_t", [P, T])
        v1 = sb("v1", [CTX, B, HEADS, HD])
        v_hl = sb("v_hl", [CTX, B, HEADS, 2, HD + 1], F16)
        kx = sb("kx", [P, 2, B * CTX], F16)
        qx = sb("qx", [P, 2, T], F16)
        k_rep = sb("k_rep", [P, BLK, B * CTX], F16)
        q_rep = sb("q_rep", [P, BLK, T], F16)
        zero_rows = sb("zero_rows", [4, BLK, T], F16)
        mx = sb("mx", [P, B, HEADS])
        mx_hl = sb("mx_hl", [P, B, 2, HEADS], F16)
        mx_t = sb("mx_t", [2 * HEADS, B * P], F16)
        prob_h = sb("prob_h", [CTX, 2, HEADS * P], F16)
        prob_l = sb("prob_l", [CTX, 2, HEADS * P], F16)
        av = sb("av", [P, HEADS, HD + 1])
        rs = sb("rs", [P, HEADS])
        ao = sb("ao", [P, B, P])
        ao_t = sb("ao_t", [P, T])
        y2 = sb("y2", [P, B, P])
        x2n = sb("x2n", [P, B, P])
        stats = sb("stats", [P, 4, B, 6])
        mv = sb("mv", [P, 4, B, 2])
        ve = sb("ve", [P, 4, B])
        rstd = sb("rstd", [P, 4, B])
        x2h = sb("x2h", [P, T], F16)
        x2l = sb("x2l", [P, T], F16)
        x2 = sb("x2", [P, B, P])
        lg = sb("lg", [P, B, E + 8])
        top = sb("top", [P, B, 8])
        cut = sb("cut", [P, B, E + 8])
        chosen = sb("chosen", [P, B, E])
        lgm = sb("lgm", [P, B, E])
        th = sb("th", [P, B, E])
        num = sb("num", [P, B, E])
        dnm = sb("dnm", [P, B, E])
        rdn = sb("rdn", [P, B, E])
        pm = sb("pm", [P, B, E])
        ps_ = sb("ps_", [P, B])
        ps2 = sb("ps2", [P, B])
        rps = sb("rps", [P, B])
        cw = sb("cw", [P, B, E])
        cw_t = sb("cw_t", [E, T])
        acc = sb("acc", [P, B, P])
        acc_all = sb("acc_all", [P, B, P])
        g32 = sb("g32", [P, 2, HALF, T])
        ghl = sb("ghl", [P, 2, RING, HALF, T], F16)
        gh, gl = ghl[:, 0], ghl[:, 1]
        stages = [w_stage[:, :], ghl[:, :, :, :, :].rearrange("p i r h t -> p (i r h t)").bitcast(F32)]
        w_high = [w1h[:, :, :].rearrange("p e n -> p (e n)"), w2h[:, :, :, :].rearrange("p e h n -> p (e h n)")]
        w_low = [w1l[:, :, :].rearrange("p e n -> p (e n)"), w2l[:, :, :, :].rearrange("p e h n -> p (e h n)")]
        fin = sb("fin", [P, B, P])

        ps = ctx.enter_context(nc.psum_tensor("ps", [P, 8, 512], F32))
        bA, bB, bC, bD, bE, bY = (ps[:, i, :] for i in range(6))
        bH = ps[:, 6:8, :]

        names = """ld_id ld_c ld_b1 ld_wide ld_xwide ld_xw ld_b ld_in ld_w1 ld_w2 ld_x ld_cx ld_swap ld_rep ld_mx st_out
            i_ones i_idb i_rows i_wt i_wtc i_b1t i_b2 i_wh i_ws i_wl i_rw i_rwl i_v1 i_lg
            x_tp x_tc q_p qg q q_cos q_sin qr kv01_p kv23_p kb v kg k_cos k_sin kr
            k_mean_p k_mean kv_p kv d_p den z out_p oz res x_beta
            st1 ag1 ve1 rs1 resg y1 st2 ag2 ve2 rs2 x1
            cx_tp cx_tc v1_p v1 vh vl x1_bo x1_tp x1_tc k_p kxh kxl q_xp qxh qxl
            s_p mx mxh mxl mxt_p mxt_c t_p prob prob_h low_pool low_dve av_p av rs_ ao
            ao_tp ao_tc wo_p y2 st3 ag3 ve3 rs3 x2n x2_tp x2h x2l
            lg_p lg top topx cut chosen lgm th num dnm rdn pm ps_ ps2 rps cw cw_tp cw_tc b2_p acc_b2
            h_p gelu hi_act hi_dve lo y_p comb st4 ag4 ve4 rs4 fin""".split()
        s = {n: sem("s_" + n) for n in names}

        def since(eng, name, n):
            if not (isinstance(n, int) and n <= 0):
                eng.wait_ge(s[name], n)

        def made_high(eng, f, e):
            mine = [i for i in range(E) if (i in HIGH_BY_ACT) == (e in HIGH_BY_ACT)]
            since(eng, "hi_act" if e in HIGH_BY_ACT else "hi_dve", len(mine) * f + mine.index(e) + 1)

        def used_high(eng, f, e):
            since(eng, "y_p", E * f + e - RING + 1)

        def first_group(f):
            return isinstance(f, int) and f == 0

        def min_groups(n):
            return min(n, GROUPS) if isinstance(n, int) else n

        x_dram = A["x"].rearrange("(g b) n c -> g n b c", b=B)
        cx_dram = A["ctx_1024"].rearrange("(g b) n c -> g n b c", b=B)
        out_dram = out.rearrange("(g b) n c -> g n b c", b=B)

        def row(name):
            return A[name].rearrange("(a n) -> a n", a=1)

        block = ctx.enter_context(nc.Block())

        @block.sync
        def _(sp):
            def load_x(a):
                since(sp, "res", a)
                since(sp, "x_beta", a)
                sp.dma_start(x[:, :, :], x_dram[a]).then_inc(s["ld_x"], 16)

            def load_cx(a):
                since(sp, "cx_tp", a)
                sp.dma_start(cx[:, :, :], cx_dram[a]).then_inc(s["ld_cx"], 16)

            def swap(a):
                since(sp, "q", a + 1)
                since(sp, "q_sin", a)
                sp.dma_start(q_swap[0::2, :], q[1::2, :]).then_inc(s["ld_swap"], 16)
                sp.dma_start(q_swap[1::2, :], q[0::2, :]).then_inc(s["ld_swap"], 16)

            def spread(a):
                since(sp, "t_p", B * a)
                sp.wait_ge(s["i_rows"], 6)
                for to, parts, low_set, high, low in ((k_rep, kx, 1, "kxh", "kxl"), (q_rep, qx, 2, "qxh", "qxl")):
                    for n in (0, 3 - low_set, low_set):
                        since(sp, low if n == low_set else high, a + 1)
                        for i in range(BLK):
                            sp.dma_start(to[n::SETS, i, :], parts[32 * i:32 * (i + 1), int(n == low_set), :]).then_inc(s["ld_rep"], 16)
                for row_at in MAX_ROWS:
                    sp.dma_start(q_rep[row_at::32, :, :], zero_rows[:, :, :]).then_inc(s["ld_rep"], 16)

            def max_rows(g):
                since(sp, "mxt_c", g + 1)
                for hl in range(2):
                    sp.dma_start(q_rep[MAX_ROWS[hl]::32, :, :], mx_t[hl * HEADS:(hl + 1) * HEADS, :]).then_inc(s["ld_mx"], 16)

            def store(f):
                since(sp, "fin", f + 1)
                sp.dma_start(out_dram[f], fin[:, :, :]).then_inc(s["st_out"], 16)

            load_x(0)
            for to, n in ((bq, "L0_attn_bq"), (xbq, "L0_xattn_bq"), (xbk, "L0_xattn_bk")):
                sp.dma_start(to[:, :], A[n].rearrange("(n a) -> n a", a=1)).then_inc(s["ld_b"], 16)
            for i, n in enumerate(("L0_attn_bk", "L0_attn_bv", "L0_attn_gamma", "L0_attn_beta")):
                sp.dma_start(wide[:, i, :], row(n).broadcast_to([P, P])).then_inc(s["ld_wide"], 16)
            load_cx(0)
            swap(0)
            load_x(1)
            load_cx(1)
            spread(0)
            for a in (1, 2):
                swap(a)
                max_rows(a - 1)
                load_x(a + 1)
                load_cx(a + 1)
                spread(a)
            with sp.Fori(3, GROUPS - 1) as a:
                swap(a)
                max_rows(a - 1)
                store(a - 3)
                load_x(a + 1)
                load_cx(a + 1)
                spread(a)
            swap(GROUPS - 1)
            max_rows(GROUPS - 2)
            store(GROUPS - 4)
            spread(GROUPS - 1)
            max_rows(GROUPS - 1)
            for f in range(GROUPS - 3, GROUPS):
                store(f)
            sp.wait_ge(s["st_out"], 16 * GROUPS)

        @block.gpsimd
        def _(pool):
            at = POOL_EARLY

            for i, n in enumerate(("L0_xattn_bv", "L0_xattn_bo")):
                pool.dma_start(wide[:, 4 + i, :], row(n).broadcast_to([P, P])).then_inc(s["ld_xwide"], 16)
            pool.dma_start(rb[:, :], row("L0_ffn_router_b").broadcast_to([P, E])).then_inc(s["ld_xwide"], 16)
            for i, n in enumerate(("L0_xattn_Wq", "L0_xattn_Wk", "L0_xattn_Wv", "L0_xattn_Wo")):
                pool.dma_start(xw[:, i, :], A[n]).then_inc(s["ld_xw"], 16)
            pool.dma_start(b2[:, :], A["L0_ffn_b2"]).then_inc(s["i_b2"], 16)
            pool.dma_start(rw[:, :], A["L0_ffn_router_w"]).then_inc(s["i_rw"], 16)
            pool.memset(q_rep[:, :, :], 0.0).then_inc(s["i_rows"], 1)
            pool.memset(zero_rows[:, :, :], 0.0).then_inc(s["i_rows"], 1)
            pool.memset(mean_col[:, :], 1.0 / P).then_inc(s["i_ones"], 1)
            pool.memset(half_pow[:, :], -0.5).then_inc(s["i_ones"], 1)
            pool.memset(v_hl[:, :, :, 0, HD:HD + 1], 1.0).then_inc(s["i_v1"], 1)
            pool.memset(v_hl[:, :, :, 1, HD:HD + 1], 0.0).then_inc(s["i_v1"], 1)
            pool.memset(lg[:, :, E:E + 8], FAR).then_inc(s["i_lg"], 1)
            pool.wait_ge(s["ld_id"], 16)
            pool.tensor_copy(ident16[:, :], ident).then_inc(s["i_idb"], 1)

            def power(n, g, name_ve, name_rs):
                since(pool, name_ve, g + 1)
                pool.tensor_tensor(rstd[:, n, :], ve[:, n, :], half_pow[:, :], ALU.pow).then_inc(s[name_rs], 1)

            def linear(a, p):
                if p == at["x_beta"]:
                    pool.wait_ge(s["ld_x"], 16 * (a + 1))
                    pool.wait_ge(s["ld_wide"], 16 * 4)
                    since(pool, "y1", a)
                    pool.tensor_tensor(x_beta[:, :, :], x[:, :, :], wide[:, 3:4, :].broadcast_to([P, B, P]), ALU.add).then_inc(s["x_beta"], 1)
                if p == at["k_rot"]:
                    since(pool, "k_sin", 2 * (a + 1))
                    since(pool, "k_cos", a + 1)
                    since(pool, "kv_p", a)
                    pool.tensor_tensor(kr[:, :, :], k_cos[:, :, :], k_sin[:, :, :], ALU.add).then_inc(s["kr"], 1)
                if p == at["q_rot"]:
                    since(pool, "q_cos", a + 1)
                    since(pool, "q_sin", a + 1)
                    since(pool, "out_p", a)
                    pool.tensor_tensor(qr[:, :], q_cos[:, :], q_sin[:, :], ALU.add).then_inc(s["qr"], 1)
                if p == at["res"]:
                    since(pool, "oz", a + 1)
                    pool.tensor_tensor(res[:, :, :], oz[:, :, :], x[:, :, :], ALU.add).then_inc(s["res"], 1)
                if p == at["norm1"]:
                    power(0, a, "ve1", "rs1")
                if p == at["norm2"]:
                    power(1, a, "ve2", "rs2")

            def entry(a, p):
                if p == at["v_low"]:
                    since(pool, "vh", a + 1)
                    pool.tensor_tensor(v_hl[:, :, :, 1, 0:HD], v1[:, :, :, :], v_hl[:, :, :, 0, 0:HD], ALU.subtract).then_inc(s["vl"], 1)

            def cross(g, p):
                if p == at["x1"]:
                    since(pool, "x1", g + 1)
                    pool.wait_ge(s["ld_xwide"], 16 * 3)
                    since(pool, "y2", g)
                    pool.tensor_tensor(x1_bo[:, :, :], x1[:, :, :], wide[:, 5:6, :].broadcast_to([P, B, P]), ALU.add).then_inc(s["x1_bo"], 1)
                for b in range(B):
                    if p == at["parts"][b]:
                        n = B * g + b
                        since(pool, "prob_h", n + 1)
                        since(pool, "av_p", n - 1)
                        c = slice(0, POOL_COLS)
                        pool.tensor_tensor(prob_l[:, b % 2, c], prob[:, b % 2, c], prob_h[:, b % 2, c], ALU.subtract).then_inc(s["low_pool"], 1)
                if p == at["x2"]:
                    power(2, g, "ve3", "rs3")

            def low_weights(p):
                for n, place in enumerate(LOW_W):
                    if p == place:
                        c = slice(n % 4 * E * HID // 4, (n % 4 + 1) * E * HID // 4)
                        pool.wait_ge(s["i_ws"], n + 1)
                        pool.tensor_tensor(w_low[n // 4][:, c], stages[n // 4][:, c], w_high[n // 4][:, c], ALU.subtract).then_inc(s["i_wl"], 1)

            def low(f, e):
                n = E * f + e
                made_high(pool, f, e)
                pool.tensor_tensor(gl[:, e % RING, :, :], g32[:, e % 2, :, :], gh[:, e % RING, :, :], ALU.subtract).then_inc(s["lo"], 1)

            def body(f, g, a):
                nonlocal at
                at = POOL_EARLY if f is None else POOL_AT
                for e in range(E):
                    for p in range(PLACES * e, PLACES * (e + 1)):
                        if f is not None and p % PLACES == at["low"]:
                            low(f, e)
                        if f is not None and p == at["finish"] and not first_group(f):
                            power(3, f - 1, "ve4", "rs4")
                        if a is not None:
                            linear(a, p)
                            entry(a, p)
                        if g is not None:
                            cross(g, p)
                        if f is None:
                            low_weights(p if g is None else p + PLACES * E)

            body(None, None, 0)
            body(None, 0, 1)
            body(0, 1, 2)
            with pool.Fori(1, GROUPS - 2) as f:
                body(f, f + 1, f + 2)
            body(GROUPS - 2, GROUPS - 1, None)
            body(GROUPS - 1, None, None)
            power(3, GROUPS - 1, "ve4", "rs4")

        @block.scalar
        def _(act):
            at = ACT_EARLY

            act.dma_start(ident, consts[:, 0:P]).then_inc(s["ld_id"], 16)
            for i, n in enumerate(("L0_attn_Wq", "L0_attn_Wk", "L0_attn_Wv")):
                act.dma_start(w_in[:, i, :], A[n]).then_inc(s["ld_in"], 16)
            act.dma_start(cst[:, P:], consts[:, P:]).then_inc(s["ld_c"], 16)
            act.dma_start(b1_in[:, :], A["L0_ffn_b1"].rearrange("e (h n) -> (e h) n", h=HALF)).then_inc(s["ld_b1"], 16)
            act.dma_start(stages[0].rearrange("p (e n) -> p e n", e=E),
                          A["L0_ffn_w1"].rearrange("e c n -> c e n")).then_inc(s["ld_w1"], 16)
            act.dma_start(stages[1].rearrange("p (e h n) -> p e h n", e=E, h=HALF),
                          A["L0_ffn_w2"].rearrange("e (h i) n -> i e h n", h=HALF)).then_inc(s["ld_w2"], 16)
            act.wait_ge(s["i_wt"], 1)
            act.copy(wq_t[:, :], bA[:, 0:P]).then_inc(s["i_wtc"], 1)
            act.copy(wkv_t[:, :, :], bA[:, P:3 * P].rearrange("p (i n) -> p i n", i=2)).then_inc(s["i_wtc"], 1)

            def high_weights(p):
                for n, place in enumerate(HIGH_W):
                    if p == place:
                        c = slice(n % 4 * E * HID // 4, (n % 4 + 1) * E * HID // 4)
                        act.wait_ge(s[("ld_w1", "ld_w2")[n // 4]], 16)
                        act.activation(w_high[n // 4][:, c], stages[n // 4][:, c], ACT.Copy, scale=WS).then_inc(s["i_wh"], 1)
                        act.wait_ge(s["i_wh"], n + 1)
                        act.activation(stages[n // 4][:, c], stages[n // 4][:, c], ACT.Copy, scale=WS).then_inc(s["i_ws"], 1)
                if p == HIGH_W[3] + 1:
                    act.wait_ge(s["ld_c"], 16)
                    for i in range(BLK):
                        act.activation(k_rep[:, i, :], cst[:, 0:B * CTX], ACT.Identity, bias=c_("max_rows"), scale=0.0).then_inc(s["i_rows"], 1)
                    act.wait_ge(s["i_rw"], 16)
                    act.activation(rwh[:, :], rw[:, :], ACT.Copy, scale=WS).then_inc(s["i_rwl"], 1)

            def linear(a, p):
                if p == at["x_t"]:
                    since(act, "x_tp", a + 1)
                    act.copy(x_t[:, :], bE).then_inc(s["x_tc"], 1)
                if p == at["q"]:
                    since(act, "q_p", a + 1)
                    act.wait_ge(s["ld_b"], 16 * 3)
                    since(act, "q", a)
                    act.activation(qg[:, :], bE, ACT.Gelu, bias=bq[:, :]).then_inc(s["qg"], 1)
                if p == at["kv23"]:
                    since(act, "kb", 2 * (a + 1))
                    since(act, "k_cos", a)
                    since(act, "k_sin", 2 * a)
                    since(act, "k_mean_p", a)
                    act.activation(kg[:, :, :], kb[:, :, :], ACT.Gelu).then_inc(s["kg"], 1)

            def entry(a, p):
                if p == at["cx_t"]:
                    since(act, "cx_tp", a + 1)
                    act.copy(cx_t[:, :], bC[:, 0:B * CTX]).then_inc(s["cx_tc"], 1)
                if p == at["x1_t"]:
                    since(act, "x1_tp", a + 1)
                    act.copy(x1_t[:, :], bC).then_inc(s["x1_tc"], 1)
                if p == at["k"]:
                    since(act, "k_p", a + 1)
                    since(act, "ld_rep", SPREAD * a)
                    act.activation(kx[:, 0, :], bD[:, 0:B * CTX], ACT.Identity, bias=xbk[:, :]).then_inc(s["kxh"], 1)
                if p == at["q_x"]:
                    since(act, "q_xp", a + 1)
                    act.activation(qx[:, 0, :], bC, ACT.Identity, bias=xbq[:, :]).then_inc(s["qxh"], 1)

            def cross(g, p):
                if p == at["max_t"]:
                    since(act, "mxt_p", g + 1)
                    since(act, "ld_mx", 2 * 16 * g)
                    act.copy(mx_t[:, :], bA[0:2 * HEADS, 0:B * P // 2].bitcast(F16)).then_inc(s["mxt_c"], 1)
                for b in range(B):
                    n = B * g + b
                    if p == at["scores_t"][b]:
                        since(act, "t_p", n + 1)
                        since(act, "low_pool", n - 1)
                        since(act, "low_dve", n - 1)
                        act.wait_ge(s["i_wl"], 4)
                        act.activation(prob[:, b % 2, :].rearrange("p (r n) -> p r n", r=4), ps[0:CTX, 0:4, :],
                                       ACT.Exp, scale=float(HD) ** -0.5).then_inc(s["prob"], 1)
                if p == at["ao_t"]:
                    since(act, "ao_tp", g + 1)
                    act.copy(ao_t[:, :], bA).then_inc(s["ao_tc"], 1)
                if p == at["x2_t"]:
                    since(act, "x2_tp", g + 1)
                    since(act, "h_p", HALF * E * g)
                    since(act, "lg_p", g)
                    act.copy(x2h[:, :], bA).then_inc(s["x2h"], 1)

            def router(f, p):
                if p == at["weights"]:
                    since(act, "lgm", f + 1)
                    act.activation(th[:, :, :], lgm[:, :, :], ACT.Tanh, scale=0.5).then_inc(s["th"], 1)
                if p == at["c_t"]:
                    since(act, "cw_tp", f + 1)
                    act.copy(cw_t[:, :], ps[0:E, 4, :]).then_inc(s["cw_tc"], 1)

            def gelu(f, e):
                n = E * f + e
                for h in range(HALF):
                    since(act, "h_p", HALF * n + h + 1)
                    if h == 0:
                        since(act, "lo", n - 1)
                    act.activation(g32[:, e % 2, h, :], bH[:, h, :], ACT.Gelu, bias=b1[:, e, h:h + 1], scale=1.0 / WS).then_inc(s["gelu"], 1)

            def high(f, e):
                since(act, "gelu", HALF * (E * f + e + 1))
                used_high(act, f, e)
                act.copy(gh[:, e % RING, :, :], g32[:, e % 2, :, :]).then_inc(s["hi_act"], 1)

            def body(f, g, a):
                nonlocal at
                at = ACT_EARLY if f is None else ACT_AT
                for e in range(E):
                    for p in range(PLACES * e, PLACES * (e + 1)):
                        if f is not None and p % PLACES == at["gelu"]:
                            gelu(f, e)
                        if f is not None and p % PLACES == at["high"] and e in HIGH_BY_ACT:
                            high(f, e)
                        if f is not None:
                            router(f, p)
                        if a is not None:
                            linear(a, p)
                            entry(a, p)
                        if g is not None:
                            cross(g, p)
                        if f is None:
                            high_weights(p if g is None else p + PLACES * E)

            body(None, None, 0)
            act.wait_ge(s["i_b1t"], 1)
            act.copy(b1[:, :, :], bA[:, 3 * P:3 * P + E * HALF].rearrange("p (e h) -> p e h", h=HALF)).then_inc(s["i_wtc"], 1)
            body(None, 0, 1)
            body(0, 1, 2)
            with act.Fori(1, GROUPS - 2) as f:
                body(f, f + 1, f + 2)
            body(GROUPS - 2, GROUPS - 1, None)
            body(GROUPS - 1, None, None)

        @block.tensor
        def _(pe):
            at = PE_EARLY
            pe.wait_ge(s["ld_id"], 16)
            pe.wait_ge(s["ld_in"], 16 * 3)
            for i in range(3):
                m = pe.transpose(bA[:, i * P:(i + 1) * P], w_in[:, i, :], ident)
            m.then_inc(s["i_wt"], 1)

            def linear(a, p):
                if p == at["x_t"]:
                    pe.wait_ge(s["ld_x"], 16 * (a + 1))
                    since(pe, "oz", a)
                    since(pe, "av", B * (a - 1))
                    since(pe, "acc_b2", a - 2)
                    for b in range(B):
                        m = pe.transpose(bE[:, b * P:(b + 1) * P], x[:, b, :], ident)
                    m.then_inc(s["x_tp"], 1)
                if p == at["q"]:
                    pe.wait_ge(s["i_wtc"], 2)
                    since(pe, "x_tc", a + 1)
                    pe.matmul(bE, wq_t[:, :], x_t[:, :], start=True, stop=True).then_inc(s["q_p"], 1)
                for j in range(2):
                    if p == at[("kv01", "kv23")[j]]:
                        if j == 0:
                            since(pe, "qg", a + 1)
                        else:
                            since(pe, "v", 2 * a + 1)
                        for b in range(2):
                            m = pe.matmul(bE[:, b * 2 * P:(b + 1) * 2 * P], x_t[:, (2 * j + b) * P:(2 * j + b + 1) * P],
                                          wkv_t[:, :, :], start=True, stop=True)
                        m.then_inc(s[("kv01_p", "kv23_p")[j]], 1)
                if p == at["k_mean"]:
                    since(pe, "kg", a + 1)
                    since(pe, "v", 2 * (a + 1))
                    pe.wait_ge(s["i_ones"], 2)
                    for b in range(B):
                        m = pe.matmul(bE[:, b:b + 1], kg[:, b, :], mean_col[:, :], start=True, stop=True)
                    m.then_inc(s["k_mean_p"], 1)
                if p == at["kv"]:
                    since(pe, "kr", a + 1)
                    since(pe, "k_mean", a + 1)
                    for b in range(B):
                        m = pe.matmul(bE[:, b * P:(b + 1) * P], kr[:, b, :], v[:, b, :], start=True, stop=True)
                    m.then_inc(s["kv_p"], 1)
                if p == at["den"]:
                    since(pe, "kv", a + 1)
                    for b in range(B):
                        m = pe.matmul(bE[:, b * HEADS:(b + 1) * HEADS], q[:, b * P:(b + 1) * P], k_mean[:, b, :], start=True, stop=True)
                    m.then_inc(s["d_p"], 1)
                if p == at["out"]:
                    since(pe, "den", a + 1)
                    since(pe, "qr", a + 1)
                    for b in range(B):
                        m = pe.matmul(bE[:, b * P:(b + 1) * P], qr[:, b * P:(b + 1) * P], kv[:, b, :], start=True, stop=True)
                    m.then_inc(s["out_p"], 1)

            def entry(a, p):
                if p == at["cx_t"]:
                    pe.wait_ge(s["ld_cx"], 16 * (a + 1))
                    since(pe, "prob", B * a)
                    for b in range(B):
                        m = pe.transpose(bC[:, b * CTX:(b + 1) * CTX], cx[:, b, :], ident[0:CTX, 0:CTX])
                    m.then_inc(s["cx_tp"], 1)
                if p == at["v1"]:
                    since(pe, "cx_tc", a + 1)
                    pe.wait_ge(s["ld_xw"], 16 * 4)
                    for b in range(B):
                        m = pe.matmul(bD[0:CTX, b * P:(b + 1) * P], cx_t[:, b * CTX:(b + 1) * CTX], xw[:, 2, :], start=True, stop=True)
                    m.then_inc(s["v1_p"], 1)
                if p == at["x1_t"]:
                    since(pe, "x1", a + 1)
                    since(pe, "cx_tc", a + 1)
                    for b in range(B):
                        m = pe.transpose(bC[:, b * P:(b + 1) * P], x1[:, b, :], ident)
                    m.then_inc(s["x1_tp"], 1)
                if p == at["k"]:
                    since(pe, "v1", a + 1)
                    pe.matmul(bD[:, 0:B * CTX], xw[:, 1, :], cx_t[:, :], start=True, stop=True).then_inc(s["k_p"], 1)
                if p == at["q_x"]:
                    since(pe, "x1_tc", a + 1)
                    pe.matmul(bC, xw[:, 0, :], x1_t[:, :], start=True, stop=True).then_inc(s["q_xp"], 1)

            def cross(g, p):
                if p == at["max_t"]:
                    since(pe, "mxl", g + 1)
                    pe.wait_ge(s["i_idb"], 1)
                    for b in range(B):
                        m = pe.transpose(bA[0:2 * HEADS, b * P // 2:(b + 1) * P // 2].bitcast(F16), mx_hl[:, b, :, :], ident16[:, :])
                    m.then_inc(s["mxt_p"], 1)
                for b in range(B):
                    if p == at["values"][b]:
                        values(g, b)
                    if p == at["scores"][b]:
                        scores(g, b)
                    if p == at["scores_t"][b]:
                        scores_t(g, b)
                if p == at["ao_t"]:
                    since(pe, "ao", B * (g + 1))
                    for b in range(B):
                        m = pe.transpose(bA[:, b * P:(b + 1) * P], ao[:, b, :], ident)
                    m.then_inc(s["ao_tp"], 1)
                if p == at["wo"]:
                    since(pe, "ao_tc", g + 1)
                    for b in range(B):
                        m = pe.matmul(bB[:, b * P:(b + 1) * P], ao_t[:, b * P:(b + 1) * P], xw[:, 3, :], start=True, stop=True)
                    m.then_inc(s["wo_p"], 1)
                if p == at["x2_t"]:
                    since(pe, "x2n", g + 1)
                    for b in range(B):
                        m = pe.transpose(bA[:, b * P:(b + 1) * P], x2n[:, b, :], ident)
                    m.then_inc(s["x2_tp"], 1)

            def scores(g, b):
                for half in range(2):
                    if b == 0:
                        since(pe, "lg", g)
                        pe.wait_ge(s["i_wtc"], 3)
                        since(pe, "ld_rep", SPREAD * (g + 1))
                    else:
                        since(pe, "mx", 2 * (B * g + b - 1) + half + 1)
                    for r in (2 * half, 2 * half + 1):
                        for i in range(BLK):
                            m = pe.matmul(ps[:, r, i * CTX:(i + 1) * CTX], q_rep[32 * r:32 * r + 32, i, b * P:(b + 1) * P],
                                          k_rep[32 * r:32 * r + 32, i, b * CTX:(b + 1) * CTX], start=True, stop=True)
                    m.then_inc(s["s_p"], 1)

            def scores_t(g, b):
                n = B * g + b
                if b == 0:
                    since(pe, "ld_mx", 2 * 16 * (g + 1))
                since(pe, "prob", n)
                for i in range(BLK):
                    for r in range(4):
                        m = pe.matmul(ps[0:CTX, r, i * P:(i + 1) * P], k_rep[32 * r:32 * r + 32, i, b * CTX:(b + 1) * CTX],
                                      q_rep[32 * r:32 * r + 32, i, b * P:(b + 1) * P], start=True, stop=True)
                m.then_inc(s["t_p"], 1)

            def values(g, b):
                n = B * g + b
                W = HD + 1
                since(pe, "low_pool", n + 1)
                since(pe, "low_dve", n + 1)
                since(pe, "vl", g + 1)
                pe.wait_ge(s["i_v1"], 2)
                if b == 0:
                    since(pe, "oz", min_groups(g + 2))
                since(pe, "av", n)
                for r in range(4):
                    for i in range(BLK):
                        c, to = (4 * r + i) * P, 2 * W * (4 * i + r)
                        pe.matmul(bE[:, to:to + 2 * W], prob_h[:, b % 2, c:c + P], v_hl[:, b, 4 * i + r, :, :], start=True, stop=False)
                        m = pe.matmul(bE[:, to:to + W], prob_l[:, b % 2, c:c + P], v_hl[:, b, 4 * i + r, 0, :], start=False, stop=True)
                m.then_inc(s["av_p"], 1)

            def router(f, p):
                if p == at["logits"]:
                    since(pe, "x2l", f + 1)
                    pe.wait_ge(s["i_rwl"], 2)
                    for b in range(B):
                        o = bA[:, b * E:(b + 1) * E]
                        xh, xl = x2h[:, b * P:(b + 1) * P], x2l[:, b * P:(b + 1) * P]
                        pe.matmul(o, xh, rwh[:, :], start=True, stop=False)
                        pe.matmul(o, xh, rwl[:, :], start=False, stop=False)
                        pe.matmul(o, xl, rwh[:, :], start=False, stop=False)
                        m = pe.matmul(o, xl, rwl[:, :], start=False, stop=True)
                    m.then_inc(s["lg_p"], 1)
                if p == at["c_t"]:
                    since(pe, "cw", f + 1)
                    since(pe, "av", B * min_groups(f + 2))
                    for b in range(B):
                        m = pe.transpose(ps[0:E, 4, b * P:(b + 1) * P], cw[:, b, :], ident)
                    m.then_inc(s["cw_tp"], 1)
                if p == at["b2"]:
                    since(pe, "cw_tc", f + 1)
                    pe.wait_ge(s["i_b2"], 16)
                    for b in range(B):
                        m = pe.matmul(bE[:, b * P:(b + 1) * P], cw_t[:, b * P:(b + 1) * P], b2[:, :], start=True, stop=True)
                    m.then_inc(s["b2_p"], 1)

            def first(f, e):
                n = E * f + e
                if e == 0:
                    since(pe, "x2l", f + 1)
                for h in range(HALF):
                    since(pe, "gelu", HALF * (n - 1) + h + 1)
                    wh, wl = w1h[:, e, h * P:(h + 1) * P], w1l[:, e, h * P:(h + 1) * P]
                    pe.matmul(bH[:, h, :], wh, x2h[:, :], start=True, stop=False)
                    pe.matmul(bH[:, h, :], wh, x2l[:, :], start=False, stop=False)
                    pe.matmul(bH[:, h, :], wl, x2h[:, :], start=False, stop=True).then_inc(s["h_p"], 1)

            def second(f, e):
                n = E * f + e
                since(pe, "lo", n + 1)
                since(pe, "comb", n)
                for b in range(B):
                    for h in range(HALF):
                        o = bY[:, b * P:(b + 1) * P]
                        ghb, glb = gh[:, e % RING, h, b * P:(b + 1) * P], gl[:, e % RING, h, b * P:(b + 1) * P]
                        pe.matmul(o, ghb, w2h[:, e, h, :], start=(h == 0), stop=False)
                        pe.matmul(o, ghb, w2l[:, e, h, :], start=False, stop=False)
                        m = pe.matmul(o, glb, w2h[:, e, h, :], start=False, stop=(h == HALF - 1))
                m.then_inc(s["y_p"], 1)

            def body(f, g, a):
                nonlocal at
                at = PE_EARLY if f is None else PE_AT
                for e in range(E):
                    for p in range(PLACES * e, PLACES * (e + 1)):
                        if f is not None and e > 0 and p % PLACES == at["next"]:
                            first(f, e)
                        if a is not None:
                            linear(a, p)
                            entry(a, p)
                        if g is not None:
                            cross(g, p)
                        if f is not None and p % PLACES == at["second"]:
                            if e >= LAG:
                                second(f, e - LAG)
                            elif not first_group(f):
                                second(f - 1, E - LAG + e)
                        if f is not None:
                            if p == at["first"]:
                                first(f, 0)
                            router(f, p)

            body(None, None, 0)
            pe.wait_ge(s["ld_b1"], 16)
            pe.wait_ge(s["i_wtc"], 2)
            pe.transpose(bA[:, 3 * P:3 * P + E * HALF], b1_in[:, :], ident[0:E * HALF, 0:E * HALF]).then_inc(s["i_b1t"], 1)
            body(None, 0, 1)
            pe.wait_ge(s["i_wl"], 8)
            body(0, 1, 2)
            with pe.Fori(1, GROUPS - 2) as f:
                body(f, f + 1, f + 2)
            body(GROUPS - 2, GROUPS - 1, None)
            body(GROUPS - 1, None, None)
            for e in range(E - LAG, E):
                second(GROUPS - 1, e)

        @block.vector
        def _(dve):
            at = DVE_EARLY

            def low_router():
                dve.wait_ge(s["i_rwl"], 1)
                dve.scalar_tensor_tensor(out=rwl[:, :], in0=rw[:, :], scalar=WS, in1=rwh[:, :], op0=ALU.mult, op1=ALU.subtract).then_inc(s["i_rwl"], 1)

            def static_wait():
                dve.wait_ge(s["ld_c"], 16)

            def wide_b(ap, n=B):
                return ap.rearrange("p (a n) -> p a n", a=1).broadcast_to([P, n, ap.shape[1]])

            def by_seq(ap):
                return ap[:, :].rearrange("p (b n) -> p b n", b=B)

            def moments(k, src, g, used, st, ag, vn, eps):
                since(dve, used, g)
                for b in range(B):
                    m = dve.bn_stats(stats[:, k, b, :], src[:, b, :])
                m.then_inc(s[st], 1)
                static_wait()
                since(dve, st, g + 1)
                for b in range(B):
                    m = dve.bn_aggr(mv[:, k, b, :], stats[:, k, b, :])
                m.then_inc(s[ag], 1)
                since(dve, ag, g + 1)
                dve.tensor_scalar(ve[:, k, :], mv[:, k, :, 1], eps, None, ALU.add).then_inc(s[vn], 1)

            def linear(a, p):
                if p == at["q"]:
                    since(dve, "qg", a + 1)
                    dve.wait_ge(s["ld_c"], 16)
                    since(dve, "ld_swap", 2 * 16 * a)
                    since(dve, "d_p", a)
                    dve.tensor_scalar(q[:, :], qg[:, :], 0.21, None, ALU.add).then_inc(s["q"], 1)
                    since(dve, "q", a + 1)
                    since(dve, "qr", a)
                    dve.tensor_tensor(by_seq(q_cos), by_seq(q), wide_b(c_("cos_t")), ALU.mult).then_inc(s["q_cos"], 1)
                for j in range(2):
                    if p == at[("kv01", "kv23")[j]]:
                        since(dve, ("kv01_p", "kv23_p")[j], a + 1)
                        since(dve, "kg", a)
                        if j == 0:
                            dve.wait_ge(s["ld_wide"], 16 * 4)
                            since(dve, "kv_p", a)
                        both = bE.rearrange("p (b i n) -> p b i n", b=2, i=2)
                        dve.tensor_tensor(kb[:, 2 * j:2 * j + 2, :], both[:, :, 0, :], wide_b(wide[:, 0, :], 2), ALU.add).then_inc(s["kb"], 1)
                        dve.tensor_tensor(v[:, 2 * j:2 * j + 2, :], both[:, :, 1, :], wide_b(wide[:, 1, :], 2), ALU.add).then_inc(s["v"], 1)
                if p == at["k_rot"]:
                    since(dve, "kg", a + 1)
                    since(dve, "kr", a)
                    dve.scalar_tensor_tensor(out=k_cos[:, :, :], in0=kg[:, :, :], scalar=0.21, in1=wide_b(c_("cos")), op0=ALU.add, op1=ALU.mult).then_inc(s["k_cos"], 1)
                    for to, name in ((0, "sin_neg"), (1, "sin")):
                        dve.scalar_tensor_tensor(out=k_sin[:, :, to::2], in0=kg[:, :, 1 - to::2], scalar=0.21, in1=wide_b(c_(name)),
                                                 op0=ALU.add, op1=ALU.mult).then_inc(s["k_sin"], 1)
                if p == at["q_sin"]:
                    since(dve, "ld_swap", 2 * 16 * (a + 1))
                    since(dve, "qr", a)
                    dve.tensor_tensor(by_seq(q_sin), by_seq(q_swap), wide_b(c_("sin_t")), ALU.mult).then_inc(s["q_sin"], 1)
                if p == at["k_mean"]:
                    since(dve, "k_mean_p", a + 1)
                    since(dve, "d_p", a)
                    dve.scalar_tensor_tensor(out=k_mean[:, :, :], in0=bE[:, 0:B].rearrange("p (b a) -> p b a", a=1).broadcast_to([P, B, HEADS]),
                                             scalar=0.21, in1=wide_b(c_("head_of")), op0=ALU.add, op1=ALU.mult).then_inc(s["k_mean"], 1)
                if p == at["kv"]:
                    since(dve, "kv_p", a + 1)
                    since(dve, "out_p", a)
                    dve.tensor_tensor(kv[:, :, :], by_seq(bE), wide_b(c_("same_head")), ALU.mult).then_inc(s["kv"], 1)
                if p == at["den"]:
                    since(dve, "d_p", a + 1)
                    dve.tensor_scalar(den[:, :], bE[:, 0:B * HEADS], 1e-6, None, ALU.add).then_inc(s["den"], 1)
                    since(dve, "den", a + 1)
                    since(dve, "oz", a)
                    dve.reciprocal(z[:, :], den[:, :]).then_inc(s["z"], 1)
                if p == at["out"]:
                    since(dve, "out_p", a + 1)
                    since(dve, "z", a + 1)
                    since(dve, "res", a)
                    dve.tensor_tensor(oz[:, :, :].rearrange("p b (h d) -> p (b h) d", d=HD), bE.rearrange("p (n d) -> p n d", d=HD),
                                      z[:, :].rearrange("p (n a) -> p n a", a=1).broadcast_to([P, B * HEADS, HD]), ALU.mult).then_inc(s["oz"], 1)
                if p == at["norm1"]:
                    since(dve, "res", a + 1)
                    moments(0, res, a, "y1", "st1", "ag1", "ve1", 1e-12)
                    for b in range(B):
                        m = dve.scalar_tensor_tensor(out=resg[:, b, :], in0=res[:, b, :], scalar=mv[:, 0, b, 0:1], in1=wide[:, 2, :],
                                                     op0=ALU.subtract, op1=ALU.mult)
                    m.then_inc(s["resg"], 1)
                if p == at["norm2"]:
                    since(dve, "rs1", a + 1)
                    since(dve, "resg", a + 1)
                    since(dve, "x_beta", a + 1)
                    since(dve, "x1", a)
                    for b in range(B):
                        m = dve.scalar_tensor_tensor(out=y1[:, b, :], in0=resg[:, b, :], scalar=rstd[:, 0, b:b + 1], in1=x_beta[:, b, :],
                                                     op0=ALU.mult, op1=ALU.add)
                    m.then_inc(s["y1"], 1)
                    since(dve, "y1", a + 1)
                    moments(1, y1, a, "x1", "st2", "ag2", "ve2", 1e-5)
                if p == at["x1"]:
                    since(dve, "rs2", a + 1)
                    since(dve, "x1_bo", a)
                    since(dve, "x1_tp", a)
                    for b in range(B):
                        m = dve.tensor_scalar(x1[:, b, :], y1[:, b, :], mv[:, 1, b, 0:1], rstd[:, 1, b:b + 1], ALU.subtract, ALU.mult)
                    m.then_inc(s["x1"], 1)

            def entry(a, p):
                if p == at["v1"]:
                    since(dve, "v1_p", a + 1)
                    dve.wait_ge(s["ld_xwide"], 16 * 3)
                    since(dve, "vl", a)
                    dve.tensor_tensor(v1[:, :, :, :].rearrange("p b h d -> p b (h d)"), bD[0:CTX, :].rearrange("p (b n) -> p b n", b=B),
                                      wide[0:CTX, 4:5, :].broadcast_to([CTX, B, P]), ALU.add).then_inc(s["v1"], 1)
                if p == at["v_high"]:
                    since(dve, "v1", a + 1)
                    since(dve, "av_p", B * a)
                    dve.tensor_copy(v_hl[:, :, :, 0, 0:HD], v1[:, :, :, :]).then_inc(s["vh"], 1)
                if p == at["k"]:
                    since(dve, "kxh", a + 1)
                    since(dve, "ld_rep", SPREAD * a)
                    dve.scalar_tensor_tensor(out=kx[:, 1, :], in0=bD[:, 0:B * CTX], scalar=xbk[:, :], in1=kx[:, 0, :],
                                             op0=ALU.add, op1=ALU.subtract).then_inc(s["kxl"], 1)
                if p == at["q_x"]:
                    since(dve, "qxh", a + 1)
                    since(dve, "ld_rep", SPREAD * a)
                    dve.scalar_tensor_tensor(out=qx[:, 1, :], in0=bC, scalar=xbq[:, :], in1=qx[:, 0, :],
                                             op0=ALU.add, op1=ALU.subtract).then_inc(s["qxl"], 1)

            def cross(g, p):
                if p == at["max"]:
                    since(dve, "mx", 2 * B * (g + 1))
                    since(dve, "mxt_p", g)
                    dve.tensor_scalar(mx_hl[:, :, 0, :], mx[:, :, :], 1.0 / MAX_SCALE, None, ALU.mult).then_inc(s["mxh"], 1)
                    since(dve, "mxh", g + 1)
                    dve.scalar_tensor_tensor(out=mx_hl[:, :, 1, :], in0=mx[:, :, :], scalar=1.0 / MAX_SCALE, in1=mx_hl[:, :, 0, :],
                                             op0=ALU.mult, op1=ALU.subtract).then_inc(s["mxl"], 1)
                for b in range(B):
                    n = B * g + b
                    if p == at["scores"][b]:
                        for half in range(2):
                            since(dve, "s_p", 2 * n + half + 1)
                            since(dve, "mxl", g)
                            dve.tensor_reduce(mx[:, b, HEADS // 2 * half:HEADS // 2 * (half + 1)].rearrange("p (r i) -> p r i", r=2),
                                              ps[:, 2 * half:2 * half + 2, 0:BLK * CTX].rearrange("p r (i k) -> p r i k", i=BLK),
                                              AX.X, ALU.max).then_inc(s["mx"], 1)
                    if p == at["parts"][b]:
                        since(dve, "prob", n + 1)
                        since(dve, "av_p", n - 1)
                        dve.tensor_copy(prob_h[:, b % 2, :], prob[:, b % 2, :]).then_inc(s["prob_h"], 1)
                        since(dve, "prob_h", n + 1)
                        c = slice(POOL_COLS, HEADS * P)
                        dve.tensor_tensor(prob_l[:, b % 2, c], prob[:, b % 2, c], prob_h[:, b % 2, c], ALU.subtract).then_inc(s["low_dve"], 1)
                    if p == at["values"][b]:
                        normalize(g, b)
                if p == at["wo"]:
                    since(dve, "wo_p", g + 1)
                    since(dve, "x1_bo", g + 1)
                    since(dve, "x2n", g)
                    dve.tensor_tensor(y2[:, :, :], by_seq(bB), x1_bo[:, :, :], ALU.add).then_inc(s["y2"], 1)
                    since(dve, "y2", g + 1)
                    moments(2, y2, g, "x2n", "st3", "ag3", "ve3", 1e-5)
                if p == at["x2"]:
                    since(dve, "rs3", g + 1)
                    since(dve, "x2_tp", g)
                    if not (isinstance(g, int) and g == 0):
                        since(dve, "comb", E * (g - 1) + 1)
                    for b in range(B):
                        m = dve.tensor_scalar(x2n[:, b, :], y2[:, b, :], mv[:, 2, b, 0:1], rstd[:, 2, b:b + 1], ALU.subtract, ALU.mult)
                    m.then_inc(s["x2n"], 1)
                if p == at["x2_t"]:
                    since(dve, "x2h", g + 1)
                    dve.tensor_tensor(x2l[:, :], bA, x2h[:, :], ALU.subtract).then_inc(s["x2l"], 1)

            def normalize(g, b):
                n = B * g + b
                W = HD + 1
                since(dve, "av_p", n + 1)
                since(dve, "ao", n)
                dve.tensor_reduce(av[:, :, :], bE[:, 0:2 * W * HEADS].rearrange("p (h t d) -> p h d t", t=2, d=W),
                                  AX.X, ALU.add).then_inc(s["av"], 1)
                since(dve, "av", n + 1)
                dve.reciprocal(rs[:, :], av[:, :, HD]).then_inc(s["rs_"], 1)
                since(dve, "rs_", n + 1)
                since(dve, "ao_tp", g)
                dve.tensor_tensor(ao[:, b, :].rearrange("p (h d) -> p h d", d=HD), av[:, :, 0:HD],
                                  rs[:, :].rearrange("p (h a) -> p h a", a=1).broadcast_to([P, HEADS, HD]), ALU.mult).then_inc(s["ao"], 1)

            def router(f, p):
                if p == at["logits"]:
                    since(dve, "lg_p", f + 1)
                    dve.wait_ge(s["i_lg"], 1)
                    since(dve, "chosen", f)
                    since(dve, "lgm", f)
                    dve.scalar_tensor_tensor(out=lg[:, :, 0:E], in0=bA[:, 0:B * E].rearrange("p (b e) -> p b e", b=B), scalar=1.0 / WS,
                                             in1=wide_b(rb[:, :]), op0=ALU.mult, op1=ALU.add).then_inc(s["lg"], 1)
                    static_wait()
                    since(dve, "lg", f + 1)
                    since(dve, "cut", f)
                    for b in range(B):
                        m = dve.max(top[:, b, :], lg[:, b, :])
                    m.then_inc(s["top"], 1)
                    since(dve, "top", f + 1)
                    since(dve, "th", f)
                    dve.tensor_tensor(lgm[:, :, :], lg[:, :, 0:E], top[:, :, 0:1].broadcast_to([P, B, E]), ALU.subtract).then_inc(s["lgm"], 1)
                    since(dve, "lgm", f + 1)
                    dve.memset(top[:, :, TOPK:8], FAR).then_inc(s["topx"], 1)
                    static_wait()
                    since(dve, "topx", f + 1)
                    for b in range(B):
                        m = dve.match_replace(cut[:, b, :], top[:, b, :], lg[:, b, :], -FAR)
                    m.then_inc(s["cut"], 1)
                    since(dve, "cut", f + 1)
                    since(dve, "pm", f)
                    dve.tensor_tensor(chosen[:, :, :], cut[:, :, 0:E], lg[:, :, 0:E], ALU.not_equal).then_inc(s["chosen"], 1)
                if p == at["weights"]:
                    since(dve, "th", f + 1)
                    since(dve, "chosen", f + 1)
                    dve.tensor_scalar(dnm[:, :, :], th[:, :, :], -1.0, 1.0, ALU.mult, ALU.add).then_inc(s["dnm"], 1)
                    dve.scalar_tensor_tensor(out=num[:, :, :], in0=th[:, :, :], scalar=1.0, in1=chosen[:, :, :], op0=ALU.add, op1=ALU.mult).then_inc(s["num"], 1)
                    since(dve, "dnm", f + 1)
                    dve.reciprocal(rdn[:, :, :], dnm[:, :, :]).then_inc(s["rdn"], 1)
                    since(dve, "rdn", f + 1)
                    since(dve, "num", f + 1)
                    dve.tensor_tensor(pm[:, :, :], num[:, :, :], rdn[:, :, :], ALU.mult).then_inc(s["pm"], 1)
                    since(dve, "pm", f + 1)
                    dve.tensor_reduce(ps_[:, :], pm[:, :, :], AX.X, ALU.add).then_inc(s["ps_"], 1)
                    since(dve, "ps_", f + 1)
                    dve.tensor_scalar(ps2[:, :], ps_[:, :], WS, None, ALU.mult).then_inc(s["ps2"], 1)
                    since(dve, "ps2", f + 1)
                    dve.reciprocal(rps[:, :], ps2[:, :]).then_inc(s["rps"], 1)
                if p == at["cw"]:
                    since(dve, "rps", f + 1)
                    since(dve, "comb", E * f)
                    since(dve, "cw_tp", f)
                    dve.tensor_tensor(cw[:, :, :], pm[:, :, :], rps[:, :].rearrange("p (b a) -> p b a", a=1).broadcast_to([P, B, E]), ALU.mult).then_inc(s["cw"], 1)
                if p == at["b2"]:
                    since(dve, "b2_p", f + 1)
                    since(dve, "comb", E * f + -((at["combine"] - p) // PLACES) - LAG)
                    dve.scalar_tensor_tensor(out=acc[:, :, :], in0=by_seq(bE), scalar=WS, in1=acc[:, :, :], op0=ALU.mult, op1=ALU.add).then_inc(s["acc_b2"], 1)

            def high(f, e):
                since(dve, "gelu", HALF * (E * f + e + 1))
                used_high(dve, f, e)
                dve.tensor_copy(gh[:, e % RING, :, :], g32[:, e % 2, :, :]).then_inc(s["hi_dve"], 1)

            def combine(f, e):
                n = E * f + e
                since(dve, "y_p", n + 1)
                if e == 0:
                    since(dve, "cw", f + 1)
                    since(dve, "x2n", f + 1)
                since(dve, "comb", n)
                since(dve, "acc_b2", f + 1 if PLACES * (e + LAG) + at["combine"] >= at["b2"] else f)
                for b in range(B):
                    m = dve.scalar_tensor_tensor(out=(acc_all if e == E - 1 else acc)[:, b, :], in0=bY[:, b * P:(b + 1) * P],
                                                 scalar=cw[:, b, e:e + 1], in1=(acc if e else x2n)[:, b, :], op0=ALU.mult, op1=ALU.add)
                m.then_inc(s["comb"], 1)

            def sum_moments(f):
                since(dve, "comb", E * (f + 1))
                moments(3, acc_all, f, "fin", "st4", "ag4", "ve4", 1e-5)

            def finish(f):
                since(dve, "rs4", f + 1)
                since(dve, "st_out", 16 * f)
                for b in range(B):
                    m = dve.tensor_scalar(fin[:, b, :], acc_all[:, b, :], mv[:, 3, b, 0:1], rstd[:, 3, b:b + 1], ALU.subtract, ALU.mult)
                m.then_inc(s["fin"], 1)

            def body(f, g, a):
                nonlocal at
                at = DVE_EARLY if f is None else DVE_AT
                for e in range(E):
                    for p in range(PLACES * e, PLACES * (e + 1)):
                        if f is not None and p % PLACES == at["high"] and e not in HIGH_BY_ACT:
                            high(f, e)
                        if f is not None:
                            router(f, p)
                        if a is not None:
                            linear(a, p)
                            entry(a, p)
                        if g is not None:
                            cross(g, p)
                        if f is not None and p % PLACES == at["combine"]:
                            if e >= LAG:
                                combine(f, e - LAG)
                            elif not first_group(f):
                                combine(f - 1, E - LAG + e)
                        if f is not None and p == at["sums"] and not first_group(f):
                            sum_moments(f - 1)
                        if f is not None and p == at["finish"] and not first_group(f):
                            finish(f - 1)

            body(None, None, 0)
            low_router()
            body(None, 0, 1)
            body(0, 1, 2)
            with dve.Fori(1, GROUPS - 2) as f:
                body(f, f + 1, f + 2)
            body(GROUPS - 2, GROUPS - 1, None)
            body(GROUPS - 1, None, None)
            for e in range(E - LAG, E):
                combine(GROUPS - 1, e)
            sum_moments(GROUPS - 1)
            finish(GROUPS - 1)


_INS = ['x', 'ctx_1024', 'L0_attn_Wq', 'L0_attn_bq', 'L0_attn_Wk', 'L0_attn_bk', 'L0_attn_Wv', 'L0_attn_bv', 'L0_attn_gamma',
        'L0_attn_beta', 'L0_xattn_Wq', 'L0_xattn_bq', 'L0_xattn_Wk', 'L0_xattn_bk', 'L0_xattn_Wv', 'L0_xattn_bv', 'L0_xattn_Wo',
        'L0_xattn_bo', 'L0_ffn_router_w', 'L0_ffn_router_b', 'L0_ffn_w1', 'L0_ffn_b1', 'L0_ffn_w2', 'L0_ffn_b2']


def kernel(**inputs):
    import numpy as _np
    import concourse.bacc as _bacc
    from concourse import mybir as _mybir
    from concourse.bass_utils import run_bass_kernel_spmd as _run

    nc = _bacc.Bacc("TRN2", target_bir_lowering=False, num_devices=1)
    arrays, aps = {}, {}
    for name in _INS:
        a = _np.ascontiguousarray(inputs[name])
        arrays[f"in_{name}"] = a
        aps[name] = nc.dram_tensor(f"in_{name}", a.shape, _mybir.dt.from_np(a.dtype), kind="ExternalInput").ap()
    table, where = constants()
    arrays["constants"] = table
    consts = nc.dram_tensor("constants", table.shape, F32, kind="ExternalInput").ap()
    out = nc.dram_tensor("out", (SEQS, P, P), F32, kind="ExternalOutput").ap()
    build(nc, aps, consts, where, out)
    r = _run(nc, [arrays], core_ids=[0])
    return r.results[0]["out"]
```
